# Optimizing a Trainium2 kernel written in Bass

```python
import numpy as np
import jax
import jax.numpy as jnp

def _softmax(x, axis=-1):
    return jax.nn.softmax(x, axis=axis)

def _gelu(x):
    return jax.nn.gelu(x, approximate=True)

def _silu(x):
    return jax.nn.silu(x)

def _sigmoid(x):
    return jax.nn.sigmoid(x)

def _layernorm(x, axis=-1, eps=1e-05):
    m = jnp.mean(x, axis=axis, keepdims=True)
    v = jnp.var(x, axis=axis, keepdims=True)
    return (x - m) / jnp.sqrt(v + eps)

def _scatter_add(tgt, idx, src, axis=0):
    return tgt.at[idx].add(src)

def _segment_sum(src, seg, n):
    return jax.ops.segment_sum(src, seg, n)
kernel_name = 'mk_adj_resnorm_d4_adj_r2_c16883'

def setup_inputs(seed: int=0):
    np.random.seed(seed)
    _w = jnp.asarray

    def _rec_inputs():
        import jax
        import jax.numpy as jnp
        _gk = jax.random.key(seed)
        x = -0.0003929 + 0.9999 * jax.random.normal(jax.random.fold_in(_gk, 1), (32, 256, 256), jnp.float32)
        _a = jax.random.bernoulli(jax.random.fold_in(_gk, 2), 0.0078125, (32, 256, 256))
        _a = jnp.logical_or(_a, jnp.eye(256, dtype=bool))
        _af = _a.astype(jnp.float32)
        _af = _af * jax.random.uniform(jax.random.fold_in(_gk, 3), (32, 256, 256), jnp.float32, 0.05, 1)
        adj = _af
        _nm = jnp.ones((32, 256), dtype=bool)
        nodemask = jnp.where(_nm, 1.0, 0.0).astype(jnp.float32)
        return (x, adj, nodemask)
    x, adj, nodemask = _rec_inputs()

    def _L0_gnn_setup():
        import jax, jax.numpy as jnp
        import numpy as np
        EPS = 1e-06
        key = jax.random.key(seed)
        k1, k2, k3 = jax.random.split(key, 3)
        B, N, F, O = (8, 2048, 256, 256)
        x = jax.random.normal(k1, (B, N, F), dtype=jnp.float32)
        adj = jax.random.uniform(k2, (B, N, N), dtype=jnp.float32)
        W = jax.random.normal(k3, (O, 2 * F), dtype=jnp.float32) * (1.0 / np.sqrt(2 * F))
        return {'x': x, 'adj': adj, 'W': W}
    _L0_gnn_all = _L0_gnn_setup()
    _L0_gnn_in = {k: v for k, v in _L0_gnn_all.items() if k in ('W',)}
    del _L0_gnn_all

    def _L1_gnn_setup():
        import jax, jax.numpy as jnp
        import numpy as np
        EPS_LN = 1e-05

        def hypergraph_conv(x, adj, W, b):
            N, C, _ = adj.shape
            H = (adj != 0).astype(x.dtype)
            w = adj.reshape(N, -1)[:, :C]
            xw = jnp.einsum('ncd,hd->nch', x, W)
            Dn = jnp.einsum('nce,ne->nc', H, w)
            Dn = jnp.where(Dn > 0, 1.0 / Dn, 0.0)
            Be = H.sum(axis=1)
            Be = jnp.where(Be > 0, 1.0 / Be, 0.0)
            m = Be[:, :, None] * jnp.einsum('nce,nch->neh', H, xw)
            out = Dn[:, :, None] * jnp.einsum('nce,neh->nch', H, m)
            return out + b

        def layer_norm(x, g, b):
            mu = jnp.mean(x, axis=-1, keepdims=True)
            var = jnp.var(x, axis=-1, keepdims=True)
            return (x - mu) * jax.lax.rsqrt(var + EPS_LN) * g + b
        key = jax.random.key(seed)
        ks = jax.random.split(key, 4)
        N, C, Din, Dh, Dout = (16, 512, 256, 512, 256)
        x = jax.random.normal(ks[0], (N, C, Din), dtype=jnp.float32)
        adj = jax.random.uniform(ks[1], (N, C, C), dtype=jnp.float32, minval=0.1, maxval=1.0)
        W1 = jax.random.normal(ks[2], (Dh, Din), dtype=jnp.float32) * (1.0 / np.sqrt(Din))
        b1 = jnp.zeros((Dh,), dtype=jnp.float32)
        gamma = jnp.ones((Dh,), dtype=jnp.float32)
        beta = jnp.zeros((Dh,), dtype=jnp.float32)
        W2 = jax.random.normal(ks[3], (Dout, Dh), dtype=jnp.float32) * (1.0 / np.sqrt(Dh))
        b2 = jnp.zeros((Dout,), dtype=jnp.float32)
        return {'x': x, 'adj': adj, 'W1': W1, 'b1': b1, 'gamma': gamma, 'beta': beta, 'W2': W2, 'b2': b2}
    _L1_gnn_all = _L1_gnn_setup()
    _L1_gnn_in = {k: v for k, v in _L1_gnn_all.items() if k in ('W1', 'b1', 'gamma', 'beta', 'W2', 'b2')}
    del _L1_gnn_all

    def _L2_gnn_setup():
        import jax, jax.numpy as jnp
        import numpy as np
        B, N, IN_DIM, ATT_DIM = (2, 4096, 256, 256)
        key = jax.random.key(seed)
        k1, k2, k3, k4 = jax.random.split(key, 4)
        X = jax.random.normal(k1, (B, N, IN_DIM), dtype=jnp.float32)
        adj = jax.random.uniform(k2, (B, N, N), dtype=jnp.float32)
        mask = jnp.ones((B, N), dtype=jnp.float32)
        Wqk = jax.random.normal(k3, (IN_DIM, 2 * ATT_DIM), dtype=jnp.float32) / np.sqrt(IN_DIM)
        Wv = jax.random.normal(k4, (IN_DIM, IN_DIM), dtype=jnp.float32) / np.sqrt(IN_DIM)
        return {'X': X, 'adj': adj, 'mask': mask, 'Wqk': Wqk, 'Wv': Wv}
    _L2_gnn_all = _L2_gnn_setup()
    _L2_gnn_in = {k: v for k, v in _L2_gnn_all.items() if k in ('Wqk', 'Wv')}
    del _L2_gnn_all

    def _L3_gnn_setup():
        import jax, jax.numpy as jnp
        import numpy as np
        B, N, DIN, DOUT, K = (4, 1024, 256, 256, 3)
        key = jax.random.key(seed)
        ks = jax.random.split(key, 8)
        X = jax.random.normal(ks[0], (B, N, DIN), dtype=jnp.float32)
        A = jax.random.uniform(ks[1], (B, N, N), dtype=jnp.float32)
        Wv = jax.random.normal(ks[2], (DIN, DOUT), dtype=jnp.float32) * 0.02
        bv = jax.random.normal(ks[3], (DOUT,), dtype=jnp.float32) * 0.02
        aw = jax.random.normal(ks[4], (2 * DOUT, 1), dtype=jnp.float32) * 0.05
        ab = jax.random.normal(ks[5], (1,), dtype=jnp.float32) * 0.05
        Wk = jax.random.normal(ks[6], (K, DIN, DOUT), dtype=jnp.float32) * 0.02
        bk = jax.random.normal(ks[7], (K, DOUT), dtype=jnp.float32) * 0.02
        return {'X': X, 'A': A, 'Wv': Wv, 'bv': bv, 'aw': aw, 'ab': ab, 'Wk': Wk, 'bk': bk}
    _L3_gnn_all = _L3_gnn_setup()
    _L3_gnn_in = {k: v for k, v in _L3_gnn_all.items() if k in ('Wv', 'bv', 'aw', 'ab', 'Wk', 'bk')}
    del _L3_gnn_all
    return {'x': x, 'adj': adj, 'nodemask': nodemask, 'L0_gnn_W': _L0_gnn_in['W'], 'L1_gnn_W1': _L1_gnn_in['W1'], 'L1_gnn_b1': _L1_gnn_in['b1'], 'L1_gnn_gamma': _L1_gnn_in['gamma'], 'L1_gnn_beta': _L1_gnn_in['beta'], 'L1_gnn_W2': _L1_gnn_in['W2'], 'L1_gnn_b2': _L1_gnn_in['b2'], 'L2_gnn_Wqk': _L2_gnn_in['Wqk'], 'L2_gnn_Wv': _L2_gnn_in['Wv'], 'L3_gnn_Wv': _L3_gnn_in['Wv'], 'L3_gnn_bv': _L3_gnn_in['bv'], 'L3_gnn_aw': _L3_gnn_in['aw'], 'L3_gnn_ab': _L3_gnn_in['ab'], 'L3_gnn_Wk': _L3_gnn_in['Wk'], 'L3_gnn_bk': _L3_gnn_in['bk']}

def reference(x, adj, nodemask, L0_gnn_W, L1_gnn_W1, L1_gnn_b1, L1_gnn_gamma, L1_gnn_beta, L1_gnn_W2, L1_gnn_b2, L2_gnn_Wqk, L2_gnn_Wv, L3_gnn_Wv, L3_gnn_bv, L3_gnn_aw, L3_gnn_ab, L3_gnn_Wk, L3_gnn_bk):
    import jax
    import jax.numpy as jnp

    def _L0_gnn_ref(x, adj, W):
        import jax, jax.numpy as jnp
        import numpy as np
        EPS = 1e-06
        deg = jnp.sum(adj, axis=-1, keepdims=True)
        agg = jnp.einsum('bij,bjf->bif', adj, x) / jnp.maximum(deg, EPS)
        cat = jnp.concatenate([x, agg], axis=2)
        out = jnp.einsum('bnf,of->bno', cat, W)
        return jax.nn.relu(out)

    def _L1_gnn_ref(x, adj, W1, b1, gamma, beta, W2, b2):
        import jax, jax.numpy as jnp
        import numpy as np
        EPS_LN = 1e-05

        def hypergraph_conv(x, adj, W, b):
            N, C, _ = adj.shape
            H = (adj != 0).astype(x.dtype)
            w = adj.reshape(N, -1)[:, :C]
            xw = jnp.einsum('ncd,hd->nch', x, W)
            Dn = jnp.einsum('nce,ne->nc', H, w)
            Dn = jnp.where(Dn > 0, 1.0 / Dn, 0.0)
            Be = H.sum(axis=1)
            Be = jnp.where(Be > 0, 1.0 / Be, 0.0)
            m = Be[:, :, None] * jnp.einsum('nce,nch->neh', H, xw)
            out = Dn[:, :, None] * jnp.einsum('nce,neh->nch', H, m)
            return out + b

        def layer_norm(x, g, b):
            mu = jnp.mean(x, axis=-1, keepdims=True)
            var = jnp.var(x, axis=-1, keepdims=True)
            return (x - mu) * jax.lax.rsqrt(var + EPS_LN) * g + b
        h = jax.nn.relu(hypergraph_conv(x, adj, W1, b1))
        h = layer_norm(h, gamma, beta)
        y = hypergraph_conv(h, adj, W2, b2)
        return y + x

    def _L2_gnn_ref(X, adj, mask, Wqk, Wv):
        import jax, jax.numpy as jnp
        import numpy as np
        B, N, IN_DIM, ATT_DIM = (2, 4096, 256, 256)
        qk = X @ Wqk
        q, k = jnp.split(qk, 2, axis=-1)
        v = X @ Wv
        att_dim = q.shape[-1]
        inv_scale = 1.0 / jnp.sqrt(jnp.float32(att_dim))
        k_m = k * mask[:, :, None]
        agg = jnp.einsum('bij,bjd->bid', adj, k_m)
        w = inv_scale * mask * jnp.einsum('bid,bid->bi', q, agg)
        L = jax.nn.softmax(w, axis=1)[:, :, None] * v
        return L

    def _L3_gnn_ref(X, A, Wv, bv, aw, ab, Wk, bk):
        import jax, jax.numpy as jnp
        import numpy as np
        B, N, DIN, DOUT, K = (4, 1024, 256, 256, 3)
        d = Wv.shape[1]
        Xw = X @ Wv + bv
        sj = Xw @ aw[:d, 0]
        si = Xw @ aw[d:, 0]
        e = jax.nn.leaky_relu(sj[:, None, :] + si[:, :, None] + ab[0], negative_slope=0.2)
        alpha_matrix = A * jnp.exp(e)
        transition = alpha_matrix / (jnp.sum(alpha_matrix, axis=-1, keepdims=True) + 1e-12)
        H = jnp.zeros(X.shape[:-1] + (d,), dtype=X.dtype)
        Xk = X
        for k in range(Wk.shape[0]):
            H = H + Xk @ Wk[k] + bk[k]
            Xk = jnp.einsum('bij,bjd->bid', transition, Xk)
        return jax.nn.relu(H)
    x = _layernorm(x + _L0_gnn_ref(x, adj, L0_gnn_W), axis=-1)
    x = _layernorm(x + _L1_gnn_ref(x, adj, L1_gnn_W1, L1_gnn_b1, L1_gnn_gamma, L1_gnn_beta, L1_gnn_W2, L1_gnn_b2), axis=-1)
    x = _layernorm(x + _L2_gnn_ref(x, adj, nodemask, L2_gnn_Wqk, L2_gnn_Wv), axis=-1)
    x = _layernorm(x + _L3_gnn_ref(x, adj, L3_gnn_Wv, L3_gnn_bv, L3_gnn_aw, L3_gnn_ab, L3_gnn_Wk, L3_gnn_bk), axis=-1)
    return x

_drawn_inputs = setup_inputs


def setup_inputs(seed=0):
    import zlib

    import numpy as np

    out = dict(_drawn_inputs(seed))
    spreads = {'L1_gnn_b1': (0.0, 0.1),
     'L1_gnn_gamma': (1.0, 0.2),
     'L1_gnn_beta': (0.0, 0.32),
     'L1_gnn_b2': (0.0, 0.1)}
    factors = {'L2_gnn_Wqk': 5.567,
     'L2_gnn_Wv': 4.476,
     'L3_gnn_Wv': 3.034,
     'L3_gnn_bv': 22.018,
     'L3_gnn_aw': 2.856}
    for name, (base, spread) in spreads.items():
        noise = np.random.default_rng([zlib.crc32(name.encode()), seed]).standard_normal(out[name].shape)
        drawn = base * np.exp(spread * noise) if base else spread * noise
        out[name] = jnp.asarray(drawn.astype(out[name].dtype))
    for name, factor in factors.items():
        out[name] = (out[name] * factor).astype(out[name].dtype)
    return out
```

```python
import concourse.bass as bass
from concourse import mybir
from contextlib import ExitStack

F32 = mybir.dt.float32
F32R = mybir.dt.float32r
ALU = mybir.AluOpType
ACT = mybir.ActivationFunctionType
AX = mybir.AxisListType

P = 128
B, N, F = 32, 256, 256
KN = N // P
KF = F // P
H1 = 512
KH = H1 // P
NO = N + 2
RING = 4
LAYERS = 4
EPS_DEG, EPS_LN, EPS_SUM = 1e-6, 1e-5, 1e-12
TINY = 1.2e-38
SLOPE = 0.2



class Batch:

    def __init__(self, i, c):
        self.i, self.c = i, c
        self.is_first = isinstance(i, int) and c == 0

    def number(self):
        return self.i * RING + self.c

    def done(self):
        return self.i * RING + (self.c + 1)

    def slot(self, ring):
        return self.c % ring

    def dma_done(self, ring):
        return self.i * (16 * RING // ring) + 16 * (self.c // ring + 1)


def steps_of(eng, step):
    head = RING
    rounds = (B - 1 - head) // RING
    for t in range(head):
        step(lambda skew, t=t: Batch(0, t - skew) if 0 <= t - skew < B else None)
    with eng.Fori(0, rounds) as i:
        for u in range(RING):
            step(lambda skew, u=u: Batch(i, head + u - skew))
    for t in range(head + rounds * RING, B + LAYERS - 1):
        step(lambda skew, t=t: Batch(0, t - skew) if 0 <= t - skew < B else None)


def resnorm_kernel(nc, at_d, xt_d, xm_d, w_l0_d, w1_d, w2_d, wqk_d, wv2_d, w3_d, wv3_d,
                   aw_d, cols_d, b2_d, bk_d, ab_d, ident_d, out_d):
    ctx = ExitStack()
    with ctx:
        def sb(name, shape, dt=F32):
            return ctx.enter_context(nc.sbuf_tensor(name, shape, dt))

        def sem(name):
            return ctx.enter_context(nc.semaphore(name))

        def sems(names):
            return [sem(n) for n in names.split()]

        ident = sb("ident", [P, P])
        ones = sb("ones", [P, P])
        eps_ln = sb("eps_ln", [P, 1])
        w3_raw = sb("w3_raw", [P, KF, 3 * F + 2])
        aw_raw = sb("aw_raw", [P, KF, 2])
        cols = sb("cols", [P, 14])
        b1c, gammac, betac, bvc = cols[:, 0:4], cols[:, 4:8], cols[:, 8:12], cols[:, 12:14]
        b2_half = sb("b2_half", [P, F])
        bk_sum = sb("bk_sum", [P, F])
        ab_b = sb("ab_b", [P, 1])
        c2 = sb("c2", [P, F])
        e_const = sb("e_const", [P, 2])
        e_bias = sb("e_bias", [P, 1])
        w0h, w0l = sb("w0h", [P, KF, 2 * F], F32R), sb("w0l", [P, KF, 2 * F], F32R)
        w1h, w1l = sb("w1h", [P, KF, H1], F32R), sb("w1l", [P, KF, H1], F32R)
        gh, gl = sb("gh", [P, KH, NO], F32R), sb("gl", [P, KH, NO], F32R)
        w2h, w2l = sb("w2h", [P, KF, 2 * F], F32R), sb("w2l", [P, KF, 2 * F], F32R)
        w3h, w3l = sb("w3h", [P, KF, 3 * F + 2], F32R), sb("w3l", [P, KF, 3 * F + 2], F32R)

        at = sb("at", [P, RING, KN, N])
        ath, atl = sb("ath", [P, RING, KN, N], F32R), sb("atl", [P, RING, KN, N], F32R)
        xt = sb("xt", [P, 2, KF, N])
        xm = sb("xm", [P, RING, KN * F + KN])

        x0th, x0tl = sb("x0th", [P, KF, N], F32R), sb("x0tl", [P, KF, N], F32R)
        t0 = sb("t0", [P, KN, F])
        zh, zl = sb("zh", [P, KN, NO], F32R), sb("zl", [P, KN, NO], F32R)
        deg, rdeg = sb("deg", [P, KN]), sb("rdeg", [P, KN])
        bn0, mv0, lv0, rs0 = sb("bn0", [P, KN, 6]), sb("mv0", [P, KN, 2]), sb("lv0", [P, KN]), sb("rs0", [P, KN])
        ht = sb("ht", [P, 2, KN, N], F32R)
        cnt, be0, be = sb("cnt", [P, KN]), sb("be0", [P, KN]), sb("be", [P, KN])
        wcol = sb("wcol", [P, KN, 2], F32R)
        dn, dpos, dmax, drec = sb("dn", [P, KN]), sb("dpos", [P, KN]), sb("dmax", [P, KN]), sb("drec", [P, KN])
        dnr = sb("dnr", [P, KN])
        dnb = sb("dnb", [P, KN, P])
        hb = sb("hb", [P, KN, N])
        hbh, hbl = sb("hbh", [P, KN, N], F32R), sb("hbl", [P, KN, N], F32R)
        x1 = sb("x1", [P, KN, F])
        x1h, x1l = sb("x1h", [P, KN, F], F32R), sb("x1l", [P, KN, F], F32R)

        sh, sl = sb("sh", [P, KN, N], F32R), sb("sl", [P, KN, N], F32R)
        sxh, sxl = sb("sxh", [P, KF, N], F32R), sb("sxl", [P, KF, N], F32R)
        r1 = sb("r1", [P, KH, N])
        r1h, r1l = sb("r1h", [P, KH, N], F32R), sb("r1l", [P, KH, N], F32R)
        sq = sb("sq", [P, KH, N])
        sq1 = sb("sq1", [P, N])
        mu1, mq1, var1, vc1 = sb("mu1", [P, KN]), sb("mq1", [P, KN]), sb("var1", [P, KN]), sb("vc1", [P, KN])
        lvh, rsh = sb("lvh", [P, KN]), sb("rsh", [P, KN])
        u = sb("u", [P, KN, F])
        uh, ul = sb("uh", [P, KN, F], F32R), sb("ul", [P, KN, F], F32R)
        t1 = sb("t1", [P, KN, F])
        bn1, mv1, lv1, rs1 = sb("bn1", [P, KN, 6]), sb("mv1", [P, KN, 2]), sb("lv1", [P, KN]), sb("rs1", [P, KN])
        x2 = sb("x2", [P, 2, KN, F])
        x2mh, x2ml = sb("x2mh", [P, KN, F], F32R), sb("x2ml", [P, KN, F], F32R)

        x2th, x2tl = sb("x2th", [P, KF, N], F32R), sb("x2tl", [P, KF, N], F32R)
        qv = sb("qv", [P, KN, 2 * F])
        wdot = sb("wdot", [P, KN])
        wb = sb("wb", [P, KN, P])
        mx, nmx = sb("mx", [P, 1]), sb("nmx", [P, 1])
        ejunk, esum, ercp = sb("ejunk", [P, N]), sb("esum", [P, 1]), sb("ercp", [P, 1])
        ew, aw = sb("ew", [P, KN]), sb("aw", [P, KN])
        t2 = qv[:, :, F:2 * F]
        bn2, mv2, lv2, rs2 = sb("bn2", [P, KN, 6]), sb("mv2", [P, KN, 2]), sb("lv2", [P, KN]), sb("rs2", [P, KN])
        x3 = sb("x3", [P, 2, KN, F])

        x3th, x3tl = sb("x3th", [P, KF, N], F32R), sb("x3tl", [P, KF, N], F32R)
        y2h, y2l = sb("y2h", [P, KN, NO], F32R), sb("y2l", [P, KN, NO], F32R)
        sj = sb("sj", [P, KN])
        sib = sb("sib", [P, KN, P])
        y01 = sb("y01", [P, KN, 2 * F])
        t3 = y01[:, :, 0:F]
        z3 = y01[:, :, F:2 * F]
        al = sb("al", [P, KN, N])
        alh, all_ = sb("alh", [P, KN, N], F32R), sb("all", [P, KN, N], F32R)
        rsum, rrec = sb("rsum", [P, KN]), sb("rrec", [P, KN])
        z3h, z3l = sb("z3h", [P, KN, F], F32R), sb("z3l", [P, KN, F], F32R)
        bn3, mv3, lv3, rs3 = sb("bn3", [P, KN, 6]), sb("mv3", [P, KN, 2]), sb("lv3", [P, KN]), sb("rs3", [P, KN])
        xo = sb("xo", [P, 2, KN, F])

        def over(tile, k):
            return tile.rearrange("p a b -> p (a b)").rearrange("p (k f) -> p k f", k=k)

        w0_raw, w1_raw = over(x3[:, 0:2, :, :].rearrange("p a b c -> p a (b c)"), KF), over(xo[:, 0:2, :, :].rearrange("p a b c -> p a (b c)"), KF)
        w2_raw, g_raw, wqk_raw, l2_raw = r1[:, :, :], sq[:, :, :], over(qv[:, :, :], KH), y01[:, :, :]
        wv3_raw, beta_b, bv_b = t1[:, :, :], over(u[:, :, :], KH), al[:, :, 0:P]
        bk_raw = over(x2[:, 0:2, :, :].rearrange("p a b c -> p a (b c)"), KH)[:, 0:3, :]
        g_mean = x1[:, 0, :]

        bank = [ctx.enter_context(nc.psum_tensor(f"bank{i}", [P, 512], F32)) for i in range(8)]
        A0, B0, A1, B1, A2, B2, A3, B3 = bank
        DN = A0[:, 264:264 + 2 * KN].rearrange("p (m c) -> p m c", c=2)

        def tiles(ps, n=KN, w=F):
            return ps[:, 0:n * w].rearrange("p (m f) -> p m f", f=w)

        def f(ap):
            return ap.bitcast(F32)

        s_w = sem("weights_loaded")
        s_memset = sem("constants_set")
        c_m, c_mean, c_c2, c_u, c_e = sems("c_m c_mean c_c2 c_u c_e")
        c_g, c_bcast, c_gc, c_l2, c_u3, c_const, c_dve, c_wready, c_act = sems(
            "c_g c_bcast c_gc c_l2 c_u3 c_const c_dve c_wready c_act")
        at_in = [sem(f"at_in{i}") for i in range(RING)]
        xt_in = [sem(f"xt_in{i}") for i in range(2)]
        xm_in = [sem(f"xm_in{i}") for i in range(RING)]
        stored = [sem(f"stored{i}") for i in range(2)]
        s_x0th, s_x0tl, s_ath, s_atl, s_ht, s_cntmax, s_be, s_wcol = sems(
            "x0th_ready x0tl_ready ath_ready atl_ready ht_ready count_clamped be_ready wcol_ready")
        s_y0mm, s_zh, s_zl, s_azmm, s_deg, s_rdeg, s_r0, s_t0 = sems(
            "y0_done zh_ready zl_ready az_done deg_ready rdeg_ready r0_ready t0_ready")
        s_bn0, s_mv0, s_lv0, s_rs0, s_x1, s_x1h, s_x1l = sems(
            "bn0_ready mv0_ready lv0_ready rs0_ready x1_ready x1h_ready x1l_ready")
        s_dnmm, s_dn, s_dpos, s_drec, s_dnr, s_dnb, s_dntr, s_hb, s_hbh, s_hbl = sems(
            "dn_done dn_ready dpos_ready drec_ready dnr_ready dnb_ready dnb_transposed hb_ready hbh_ready hbl_ready")
        s_smm, s_sh, s_sl, s_sxmm, s_sxh, s_sxl, s_rmm, s_r1, s_r1h, s_r1l = sems(
            "s_done sh_ready sl_ready sx_done sxh_ready sxl_ready r_done r1_ready r1h_ready r1l_ready")
        s_sq, s_sq2, s_sq1, s_vmm, s_mu, s_mq, s_var, s_vc, s_lvh, s_rsh = sems(
            "sq_ready sq2_ready sq1_ready v_done mu_ready mq_ready var_ready varc_ready lvh_ready rsh_ready")
        s_u, s_uh, s_ul, s_x1b, s_ymm, s_t1, s_bn1, s_mv1, s_lv1, s_rs1, s_x2, s_x2mh, s_x2ml = sems(
            "u_ready uh_ready ul_ready x1b_ready y_done t1_ready bn1_ready mv1_ready lv1_ready rs1_ready "
            "x2_ready x2mh_ready x2ml_ready")
        s_x2tr, s_x2th, s_x2tl, s_qvmm, s_qv, s_aggmm, s_w2, s_wb, s_wtr, s_mx, s_nmx, s_esum, s_ercp, s_a = sems(
            "x2_transposed x2th_ready x2tl_ready qv_done qv_ready agg_done w_ready wb_ready w_transposed "
            "max_ready negmax_ready exps_ready ercp_ready a_ready")
        s_t2, s_bn2, s_mv2, s_lv2, s_rs2, s_x3 = sems("t2_ready bn2_ready mv2_ready lv2_ready rs2_ready x3_ready")
        s_x3tr, s_x3th, s_x3tl, s_y2mm, s_y2h, s_y2l, s_sib, s_sitr, s_ez, s_el, s_ee, s_al, s_alh, s_all = sems(
            "x3_transposed x3th_ready x3tl_ready y2_done y2h_ready y2l_ready sib_ready si_transposed "
            "ez_ready el_ready ee_ready alpha_ready alh_ready all_ready")
        s_y01mm, s_y01, s_y0b, s_p2mm, s_rsum, s_rrec, s_z3, s_z3h, s_z3l, s_p1mm, s_r3, s_t3 = sems(
            "y01_done y01_ready y0b_ready p2_done rowsum_ready rrec_ready z3_ready z3h_ready z3l_ready "
            "p1_done r3_ready t3_ready")
        s_bn3, s_mv3, s_lv3, s_rs3, s_xo = sems("bn3_ready mv3_ready lv3_ready rs3_ready out_ready")

        s_r1h2 = sem("r1h_half_ready")

        def mask_of(b, m):
            return xm[:, b.slot(RING), KN * F + m:KN * F + m + 1]

        def ready(eng, s, b):
            eng.wait_ge(s, b.done())

        def reuse(eng, s, b):
            if not b.is_first:
                eng.wait_ge(s, b.number())

        block = ctx.enter_context(nc.Block())

        n_weights = 13

        @block.sync
        def _(sp):
            def load_at(b):
                sp.dma_start(at[:, b.slot(RING), :, :], at_d[b.number(), :, :, :]).then_inc(at_in[b.slot(RING)], 16)

            def load_xt(b):
                sp.dma_start(xt[:, b.slot(2), :, :], xt_d[b.number(), :, :, :]).then_inc(xt_in[b.slot(2)], 16)

            def load_xm(b):
                sp.dma_start(xm[:, b.slot(RING), :], xm_d[b.number(), :, :]).then_inc(xm_in[b.slot(RING)], 16)

            sp.dma_start(w0_raw, w_l0_d).then_inc(s_w, 16)
            first = Batch(0, 0)
            load_xt(first)
            load_at(first)
            load_xm(first)
            for dst, src in ((cols[:, :], cols_d), (w1_raw, w1_d), (w2_raw, w2_d),
                             (ident[:, :], ident_d), (wqk_raw, wqk_d),
                             (l2_raw[:, :, F:2 * F], wv2_d), (w3_raw[:, :, 0:3 * F], w3_d),
                             (wv3_raw, wv3_d), (aw_raw[:, :, :], aw_d), (b2_half[:, :], b2_d),
                             (bk_raw, bk_d), (ab_b[:, :], ab_d)):
                sp.dma_start(dst, src).then_inc(s_w, 16)

            def step(of):
                nxt, b3 = of(-1), of(3)
                if nxt:
                    if not (isinstance(nxt.i, int) and nxt.c < 2):
                        sp.wait_ge(s_x0tl, nxt.number() - 1)
                    load_xt(nxt)
                    if not (isinstance(nxt.i, int) and nxt.c < RING):
                        sp.wait_ge(s_w2, nxt.number() - (RING - 1))
                        sp.wait_ge(s_x2ml, nxt.number() - (RING - 1))
                    load_xm(nxt)
                if b3:
                    ready(sp, s_al, b3)
                if nxt:
                    load_at(nxt)
                if b3:
                    ready(sp, s_xo, b3)
                    sp.dma_start(out_d[b3.number(), :, :, :], xo[:, b3.slot(2), :, :]).then_inc(stored[b3.slot(2)], 16)

            steps_of(sp, step)
            for s in stored:
                sp.wait_ge(s, 16 * B // 2)

        @block.tensor
        def _(pe):
            def mm(out, lhs, rhs, start, stop):
                return nc.tensor.matmul(out, lhs, rhs, start=start, stop=stop)

            def product(out, lhs, rhs, k_tiles):
                for k in range(k_tiles):
                    (lh, ll), (rh, rl) = lhs(k), rhs(k)
                    mm(out, lh, rh, k == 0, False)
                    mm(out, lh, rl, False, False)
                    last = mm(out, ll, rh, False, k == k_tiles - 1)
                return last

            def cut(m):
                return slice(m * P, (m + 1) * P)

            def transposes(ps, src):
                for m in range(KN):
                    for k in range(KF):
                        last = nc.tensor.transpose(tiles(ps)[:, k, cut(m)], src[:, m, cut(k)], ident[:, :])
                return last

            def constants():
                pe.wait_ge(s_w, 16 * n_weights)
                for m in range(KF):
                    for k in range(KF):
                        last = mm(tiles(A2)[:, m, :], wqk_raw[:, k, cut(m)], wqk_raw[:, KF + k, :], k == 0, k == KF - 1)
                last.then_inc(c_m, 1)
                pe.wait_ge(c_g, 1)
                pe.wait_ge(s_memset, 1)
                for k in range(KH):
                    last = mm(A1[:, 0:F], ones[:, :], g_raw[:, k, :], k == 0, k == KH - 1)
                last.then_inc(c_mean, 1)
                pe.wait_ge(c_bcast, 1)
                for k in range(KH):
                    last = mm(B1[:, 0:F], beta_b[:, k, :], w2_raw[:, k, :], k == 0, k == KH - 1)
                last.then_inc(c_c2, 1)
                for m in range(KF):
                    for k in range(KF):
                        last = mm(A3[:, 2 * m:2 * m + 2], wv3_raw[:, k, cut(m)], aw_raw[:, k, :], k == 0, k == KF - 1)
                last.then_inc(c_u, 1)
                for k in range(KF):
                    last = mm(B3[:, 0:2], bv_b[:, k, :], aw_raw[:, k, :], k == 0, k == KF - 1)
                last.then_inc(c_e, 1)

            def l0_y(b):
                ready(pe, s_x0tl, b)
                ready(pe, s_x0th, b)
                reuse(pe, s_r0, b)
                reuse(pe, s_hb, b)
                for m, ps in enumerate((A0, B0)):
                    last = product(ps[:, :], lambda k: (x0th[:, k, cut(m)], x0tl[:, k, cut(m)]),
                                   lambda k: (w0h[:, k, :], w0l[:, k, :]), KF)
                    last.then_inc(s_y0mm, 1)

            def l0_az(b):
                s = b.slot(RING)
                ready(pe, s_zl, b)
                ready(pe, s_atl, b)
                ready(pe, s_ath, b)
                for m, ps in enumerate((A0, B0)):
                    last = product(ps[:, 0:NO], lambda k: (ath[:, s, k, cut(m)], atl[:, s, k, cut(m)]),
                                   lambda k: (zh[:, k, :], zl[:, k, :]), KN)
                last.then_inc(s_azmm, 1)

            def l0_dn(b):
                h = b.slot(2)
                ready(pe, s_zl, b)
                ready(pe, s_ht, b)
                ready(pe, s_wcol, b)
                for m in range(KN):
                    for k in range(KN):
                        last = mm(DN[:, m, :], ht[:, h, k, cut(m)], wcol[:, k, :], k == 0, k == KN - 1)
                last.then_inc(s_dnmm, 1)

            def l0_dn_rows(b):
                ready(pe, s_dnb, b)
                ready(pe, s_r0, b)
                for m in range(KN):
                    last = nc.tensor.transpose(B0[:, cut(m)], dnb[:, m, :], ident[:, :])
                last.then_inc(s_dntr, 1)

            def l1_s(b):
                h = b.slot(2)
                ready(pe, s_hbl, b)
                ready(pe, s_hbh, b)
                ready(pe, s_ht, b)
                reuse(pe, s_t1, b)
                for m in range(KN):
                    for k in range(KN):
                        mm(tiles(A1)[:, m, :], ht[:, h, k, cut(m)], hbh[:, k, :], k == 0, False)
                        last = mm(tiles(A1)[:, m, :], ht[:, h, k, cut(m)], hbl[:, k, :], False, k == KN - 1)
                last.then_inc(s_smm, 1)

            def l1_sx(b):
                ready(pe, s_sl, b)
                ready(pe, s_sh, b)
                ready(pe, s_x1l, b)
                ready(pe, s_x1h, b)
                reuse(pe, s_u, b)
                for m in range(KF):
                    last = product(tiles(B1)[:, m, :], lambda k: (x1h[:, k, cut(m)], x1l[:, k, cut(m)]),
                                   lambda k: (sh[:, k, :], sl[:, k, :]), KN)
                last.then_inc(s_sxmm, 1)

            def l1_r(b):
                ready(pe, s_sxl, b)
                ready(pe, s_sxh, b)
                for m in range(KH):
                    last = product(tiles((A1, B1)[m // 2])[:, m % 2, :],
                                   lambda k: (w1h[:, k, cut(m)], w1l[:, k, cut(m)]),
                                   lambda k: (sxh[:, k, :], sxl[:, k, :]), KF)
                    if m % 2:
                        last.then_inc(s_rmm, 1)

            def l1_v(b):
                ready(pe, s_r1l, b)
                for m, ps in enumerate((A1, B1)):
                    product(ps[:, 0:NO], lambda k: (r1h[:, k, cut(m)], r1l[:, k, cut(m)]),
                            lambda k: (gh[:, k, :], gl[:, k, :]), KH)
                ready(pe, s_sq1, b)
                for m, ps in enumerate((A1, B1)):
                    last = mm(ps[:, NO:NO + 1], sq1[:, cut(m)], ones[:, 0:1], True, True)
                last.then_inc(s_vmm, 1)

            def l1_y(b):
                ready(pe, s_ul, b)
                ready(pe, s_uh, b)
                for m in range(KN):
                    last = product(tiles(A1)[:, m, :], lambda k: (sh[:, k, cut(m)], sl[:, k, cut(m)]),
                                   lambda k: (uh[:, k, :], ul[:, k, :]), KN)
                last.then_inc(s_ymm, 1)

            def l2_tr(b):
                ready(pe, s_x2, b)
                reuse(pe, s_esum, b)
                transposes(A2, x2[:, b.slot(2), :, :]).then_inc(s_x2tr, 1)

            def l2_qv(b):
                ready(pe, s_x2tl, b)
                ready(pe, s_x2th, b)
                reuse(pe, s_w2, b)
                for m, ps in enumerate((B2, A2)):
                    last = product(ps[:, :], lambda k: (x2th[:, k, cut(m)], x2tl[:, k, cut(m)]),
                                   lambda k: (w2h[:, k, :], w2l[:, k, :]), KF)
                    last.then_inc(s_qvmm, 1)

            def l2_agg(b):
                s = b.slot(RING)
                ready(pe, s_x2ml, b)
                ready(pe, s_x2mh, b)
                ready(pe, s_qv, b)
                for m in range(KN):
                    last = product(tiles(B2)[:, m, :], lambda k: (ath[:, s, k, cut(m)], atl[:, s, k, cut(m)]),
                                   lambda k: (x2mh[:, k, :], x2ml[:, k, :]), KN)
                last.then_inc(s_aggmm, 1)

            def l2_w_rows(b):
                ready(pe, s_wb, b)
                for m in range(KN):
                    last = nc.tensor.transpose(A2[:, cut(m)], wb[:, m, :], ident[:, :])
                last.then_inc(s_wtr, 1)

            def l3_tr(b):
                ready(pe, s_x3, b)
                reuse(pe, s_r3, b)
                transposes(A3, x3[:, b.slot(2), :, :]).then_inc(s_x3tr, 1)

            def l3_y2(b):
                ready(pe, s_x3tl, b)
                ready(pe, s_x3th, b)
                reuse(pe, s_z3, b)
                for m, ps in enumerate((B3, A3)):
                    last = product(ps[:, 0:NO], lambda k: (x3th[:, k, cut(m)], x3tl[:, k, cut(m)]),
                                   lambda k: (w3h[:, k, 2 * F:3 * F + 2], w3l[:, k, 2 * F:3 * F + 2]), KF)
                    last.then_inc(s_y2mm, 1)

            def l3_si_rows(b):
                ready(pe, s_sib, b)
                ready(pe, s_y2l, b)
                for m in range(KN):
                    last = nc.tensor.transpose(B3[:, cut(m)], sib[:, m, :], ident[:, :])
                last.then_inc(s_sitr, 1)

            def l3_y01(b):
                ready(pe, s_y2l, b)
                ready(pe, s_ez, b)
                for m, ps in enumerate((A3, B3)):
                    last = product(ps[:, :], lambda k: (x3th[:, k, cut(m)], x3tl[:, k, cut(m)]),
                                   lambda k: (w3h[:, k, 0:2 * F], w3l[:, k, 0:2 * F]), KF)
                    last.then_inc(s_y01mm, 1)

            def l3_p2(b):
                ready(pe, s_all, b)
                ready(pe, s_alh, b)
                ready(pe, s_y2h, b)
                ready(pe, s_y01, b)
                for m, ps in enumerate((A3, B3)):
                    last = product(ps[:, 0:NO], lambda k: (alh[:, k, cut(m)], all_[:, k, cut(m)]),
                                   lambda k: (y2h[:, k, :], y2l[:, k, :]), KN)
                last.then_inc(s_p2mm, 1)

            def l3_p1(b):
                ready(pe, s_z3l, b)
                ready(pe, s_z3h, b)
                for m in range(KN):
                    last = product(tiles(A3)[:, m, :], lambda k: (alh[:, k, cut(m)], all_[:, k, cut(m)]),
                                   lambda k: (z3h[:, k, :], z3l[:, k, :]), KN)
                last.then_inc(s_p1mm, 1)

            def step(of):
                b0, b1, b2, b3 = of(0), of(1), of(2), of(3)
                for stage, b in ((l0_y, b0), (l1_s, b1), (l3_tr, b3), (l2_tr, b2), (l1_sx, b1), (l3_y2, b3),
                                 (l2_qv, b2), (l3_si_rows, b3), (l2_agg, b2), (l1_r, b1), (l0_dn, b0), (l0_az, b0),
                                 (l3_y01, b3), (l2_w_rows, b2), (l3_p2, b3), (l0_dn_rows, b0), (l1_v, b1),
                                 (l3_p1, b3), (l1_y, b1)):
                    if b:
                        stage(b)

            pe.wait_ge(c_wready, 1)
            constants()
            pe.wait_ge(c_const, 1)
            steps_of(pe, step)

        @block.scalar
        def _(act):
            def copy(out, src, **kw):
                return nc.scalar.activation(out, src, ACT.Identity, **kw)

            def rstd(lv, rs, mv, s_mv, s_lv, s_rs, b):
                ready(act, s_mv, b)
                nc.scalar.activation(lv[:, :], mv, ACT.Ln, bias=eps_ln[:, 0:1]).then_inc(s_lv, 1)
                ready(act, s_lv, b)
                nc.scalar.activation(rs[:, :], lv[:, :], ACT.Exp, scale=-0.5).then_inc(s_rs, 1)

            def constants():
                act.wait_ge(s_w, 16 * n_weights)
                copy(w0h[:, :, :], w0_raw)
                copy(w1h[:, :, :], w1_raw).then_inc(c_act, 1)
                act.wait_ge(c_gc, 1)
                copy(gh[:, :, 0:F], g_raw[:, :, :]).then_inc(c_act, 1)
                act.wait_ge(c_l2, 1)
                copy(w2h[:, :, :], l2_raw[:, :, :]).then_inc(c_act, 1)
                act.wait_ge(c_u3, 1)
                copy(w3h[:, :, :], w3_raw[:, :, :]).then_inc(c_act, 1)

            def l0_split_x(b):
                act.wait_ge(xt_in[b.slot(2)], b.dma_done(2))
                reuse_c = Batch(b.i, b.c)
                if not reuse_c.is_first:
                    act.wait_ge(s_y0mm, b.number() * KN)
                copy(x0th[:, :, :], xt[:, b.slot(2), :, :]).then_inc(s_x0th, 1)

            def l0_split_at(b):
                s = b.slot(RING)
                act.wait_ge(at_in[s], b.dma_done(RING))
                copy(ath[:, s, :, :], at[:, s, :, :]).then_inc(s_ath, 1)

            def l0_z(b):
                for m, ps in enumerate((A0, B0)):
                    act.wait_ge(s_y0mm, b.number() * KN + m + 1)
                    if m == 0:
                        reuse(act, s_azmm, b)
                        reuse(act, s_x1, b)
                    copy(zh[:, m, 0:F], ps[:, F:2 * F])
                    copy(t0[:, m, :], ps[:, 0:F]).then_inc(s_zh, 1)

            def l0_rstd(b):
                rstd(lv0, rs0, mv0[:, :, 1], s_mv0, s_lv0, s_rs0, b)

            def l0_x1h(b):
                ready(act, s_x1, b)
                reuse(act, s_sxmm, b)
                copy(x1h[:, :, :], x1[:, :, :]).then_inc(s_x1h, 1)

            def l0_hbh(b):
                ready(act, s_hb, b)
                reuse(act, s_smm, b)
                copy(hbh[:, :, :], hb[:, :, :]).then_inc(s_hbh, 1)

            def l1_sh(b):
                ready(act, s_smm, b)
                reuse(act, s_ymm, b)
                copy(sh[:, :, :], tiles(A1)).then_inc(s_sh, 1)

            def l1_sxh(b):
                ready(act, s_sxmm, b)
                act.wait_ge(s_rmm, b.number() * 2) if not b.is_first else None
                copy(sxh[:, :, :], tiles(B1)).then_inc(s_sxh, 1)

            def l1_r1(b):
                reuse(act, s_r1l, b)
                reuse(act, s_sq, b)
                for m in range(KH):
                    if m % 2 == 0:
                        act.wait_ge(s_rmm, b.number() * 2 + m // 2 + 1)
                    last = nc.scalar.activation(r1[:, m, :], tiles((A1, B1)[m // 2])[:, m % 2, :], ACT.Relu,
                                                bias=b1c[:, m:m + 1])
                    if m % 2:
                        last.then_inc(s_r1, 1)

            def l1_r1h(b):
                reuse(act, s_vmm, b)
                for m in range(2):
                    act.wait_ge(s_r1, b.number() * 2 + m + 1)
                    copy(r1h[:, 2 * m:2 * m + 2, :], r1[:, 2 * m:2 * m + 2, :]).then_inc(s_r1h2, 1)

            def l1_hidden_rstd(b):
                rstd(lvh, rsh, vc1[:, :], s_vc, s_lvh, s_rsh, b)

            def l1_uh(b):
                ready(act, s_u, b)
                reuse(act, s_ymm, b)
                copy(uh[:, :, :], u[:, :, :]).then_inc(s_uh, 1)

            def l1_rstd(b):
                rstd(lv1, rs1, mv1[:, :, 1], s_mv1, s_lv1, s_rs1, b)

            def l1_x2mh(b):
                ready(act, s_x2, b)
                reuse(act, s_aggmm, b)
                for m in range(KN):
                    last = copy(x2mh[:, m, :], x2[:, b.slot(2), m, :], scale=mask_of(b, m))
                last.then_inc(s_x2mh, 1)

            def l2_x2th(b):
                ready(act, s_x2tr, b)
                if not b.is_first:
                    act.wait_ge(s_qvmm, b.number() * KN)
                copy(x2th[:, :, :], tiles(A2)).then_inc(s_x2th, 1)

            def l2_qv(b):
                reuse(act, s_x3, b)
                for m, ps in enumerate((B2, A2)):
                    act.wait_ge(s_qvmm, b.number() * KN + m + 1)
                    last = copy(qv[:, m, :], ps[:, :])
                last.then_inc(s_qv, 1)

            def l2_exp(b):
                ready(act, s_nmx, b)
                nc.scalar.activation(ew[:, :], wdot[:, :], ACT.Exp, bias=nmx[:, 0:1])
                nc.scalar.activation(ejunk[:, :], A2[:, 0:N], ACT.Exp, bias=nmx[:, 0:1],
                                     accum_out=esum[:, 0:1]).then_inc(s_esum, 1)

            def l2_rstd(b):
                rstd(lv2, rs2, mv2[:, :, 1], s_mv2, s_lv2, s_rs2, b)

            def l3_x3th(b):
                ready(act, s_x3tr, b)
                if not b.is_first:
                    act.wait_ge(s_y01mm, b.number() * KN)
                copy(x3th[:, :, :], tiles(A3)).then_inc(s_x3th, 1)

            def l3_y2h(b):
                reuse(act, s_p2mm, b)
                for m, ps in enumerate((B3, A3)):
                    act.wait_ge(s_y2mm, b.number() * KN + m + 1)
                    last = copy(y2h[:, m, 0:F], ps[:, 0:F])
                last.then_inc(s_y2h, 1)

            def l3_ez(b):
                ready(act, s_sitr, b)
                reuse(act, s_all, b)
                for m in range(KN):
                    last = copy(al[:, m, :], B3[:, 0:N], bias=sj[:, m:m + 1])
                last.then_inc(s_ez, 1)

            def l3_exp(b):
                ready(act, s_el, b)
                nc.scalar.activation(al[:, :, :], al[:, :, :], ACT.Exp).then_inc(s_ee, 1)

            def l3_alh(b):
                ready(act, s_al, b)
                reuse(act, s_p1mm, b)
                copy(alh[:, :, :], al[:, :, :]).then_inc(s_alh, 1)

            def l3_y01(b):
                reuse(act, s_z3l, b)
                reuse(act, s_xo, b)
                for m, ps in enumerate((A3, B3)):
                    act.wait_ge(s_y01mm, b.number() * KN + m + 1)
                    last = copy(y01[:, m, :], ps[:, :])
                last.then_inc(s_y01, 1)

            def l3_z3h(b):
                ready(act, s_z3, b)
                reuse(act, s_p1mm, b)
                copy(z3h[:, :, :], z3).then_inc(s_z3h, 1)

            def l3_rstd(b):
                rstd(lv3, rs3, mv3[:, :, 1], s_mv3, s_lv3, s_rs3, b)

            def step(of):
                bn, b0, b1, b2, b3 = of(-1), of(0), of(1), of(2), of(3)
                for stage, b in ((l0_split_at, b0), (l0_z, b0), (l1_sh, b1), (l3_x3th, b3), (l2_x2th, b2),
                                 (l1_sxh, b1), (l3_y2h, b3), (l3_ez, b3), (l2_qv, b2), (l3_exp, b3), (l3_alh, b3),
                                 (l1_r1, b1), (l1_r1h, b1), (l2_exp, b2), (l0_rstd, b0), (l3_y01, b3),
                                 (l2_rstd, b2), (l0_x1h, b0), (l3_z3h, b3), (l1_hidden_rstd, b1), (l0_hbh, b0),
                                 (l0_split_x, bn), (l1_uh, b1), (l3_rstd, b3), (l1_rstd, b1), (l1_x2mh, b1)):
                    if b:
                        stage(b)

            nc.scalar.preload_act_table_set("natural_log_exp_and_others")
            constants()
            l0_split_x(Batch(0, 0))
            steps_of(act, step)

        @block.vector
        def _(dve):
            v = nc.vector

            def layer_norm(t, bn, mv, rs, out, s_t, s_bn, s_mv, s_rs, s_out, b):
                ready(dve, s_t, b)
                for m in range(KN):
                    last = v.bn_stats(bn[:, m, :], t[:, m, :])
                last.then_inc(s_bn, 1)
                dve.wait_ge(s_memset, 1)
                ready(dve, s_bn, b)
                for m in range(KN):
                    last = v.bn_aggr(mv[:, m, :], bn[:, m, :])
                last.then_inc(s_mv, 1)

            def normalise(t, mv, rs, out, s_rs, s_out, b):
                ready(dve, s_rs, b)
                for m in range(KN):
                    last = v.tensor_scalar(out[:, m, :], t[:, m, :], mv[:, m, 0:1], rs[:, m:m + 1],
                                           ALU.subtract, ALU.mult)
                last.then_inc(s_out, 1)

            def low(out, whole, high):
                return v.tensor_tensor(out, whole, f(high), ALU.subtract)

            def constants():
                v.memset(ones[:, :], 1.0)
                v.memset(eps_ln[:, :], EPS_LN).then_inc(s_memset, 1)
                for t, val in ((zh, 1.0), (zl, 0.0), (y2h, 1.0), (y2l, 0.0), (gh, 1.0), (gl, 0.0)):
                    v.memset(f(t[:, :, F:NO]), val)
                dve.wait_ge(s_w, 16 * n_weights)
                for k in range(KH):
                    last = v.tensor_scalar(g_raw[:, k, :], w2_raw[:, k, :], gammac[:, k:k + 1], None, ALU.mult)
                last.then_inc(c_g, 1)
                dve.wait_ge(s_memset, 1)
                for k in range(KH):
                    v.tensor_scalar(beta_b[:, k, :], ones[:, :], betac[:, k:k + 1], None, ALU.mult)
                for k in range(KF):
                    last = v.tensor_scalar(bv_b[:, k, :], ones[:, :], bvc[:, k:k + 1], None, ALU.mult)
                last.then_inc(c_bcast, 1)
                dve.wait_ge(c_act, 1)
                low(w0l[:, :, :], w0_raw, w0h[:, :, :]).then_inc(c_wready, 1)
                low(w1l[:, :, :], w1_raw, w1h[:, :, :])
                dve.wait_ge(c_m, 1)
                v.tensor_scalar(l2_raw[:, :, 0:F], tiles(A2), float(F) ** -0.5, None, ALU.mult).then_inc(c_l2, 1)
                dve.wait_ge(c_mean, 1)
                v.tensor_scalar(g_mean, A1[:, 0:F], 1.0 / H1, None, ALU.mult).then_inc(c_dve, 1)
                dve.wait_ge(c_dve, 1)
                dve.wait_ge(c_g, 1)
                for k in range(KH):
                    last = v.tensor_tensor(g_raw[:, k, :], g_raw[:, k, :], g_mean, ALU.subtract)
                last.then_inc(c_gc, 1)
                dve.wait_ge(c_c2, 1)
                v.tensor_copy(c2[:, :], B1[:, 0:F])
                dve.wait_ge(c_u, 1)
                for m in range(KF):
                    last = v.tensor_copy(w3_raw[:, m, 3 * F:3 * F + 2], A3[:, 2 * m:2 * m + 2])
                last.then_inc(c_u3, 1)
                dve.wait_ge(c_e, 1)
                v.tensor_copy(e_const[:, :], B3[:, 0:2])
                v.tensor_scalar(b2_half[:, :], b2_half[:, :], 0.5, None, ALU.mult)
                v.tensor_tensor(bk_sum[:, :], bk_raw[:, 0, :], bk_raw[:, 1, :], ALU.add).then_inc(c_dve, 1)
                dve.wait_ge(c_dve, 2)
                v.tensor_tensor(e_bias[:, :], e_const[:, 0:1], e_const[:, 1:2], ALU.add)
                v.tensor_tensor(bk_sum[:, :], bk_sum[:, :], bk_raw[:, 2, :], ALU.add).then_inc(c_dve, 1)
                dve.wait_ge(c_dve, 3)
                v.tensor_tensor(e_bias[:, :], e_bias[:, :], ab_b[:, :], ALU.add)
                dve.wait_ge(c_act, 2)
                low(gl[:, :, 0:F], g_raw[:, :, :], gh[:, :, 0:F])
                dve.wait_ge(c_act, 3)
                dve.wait_ge(c_l2, 1)
                low(w2l[:, :, :], l2_raw[:, :, :], w2h[:, :, :])
                dve.wait_ge(c_act, 4)
                dve.wait_ge(c_u3, 1)
                low(w3l[:, :, :], w3_raw[:, :, :], w3h[:, :, :]).then_inc(c_const, 1)

            def l0_split_x(b):
                ready(dve, s_x0th, b)
                low(x0tl[:, :, :], xt[:, b.slot(2), :, :], x0th[:, :, :]).then_inc(s_x0tl, 1)

            def l0_h(b):
                s, h = b.slot(RING), b.slot(2)
                dve.wait_ge(at_in[s], b.dma_done(RING))
                for k in range(KN):
                    last = v.tensor_scalar(ht[:, h, k, :], at[:, s, k, :], 0.0, None, ALU.not_equal, ALU.add,
                                           accum_out=cnt[:, k:k + 1])
                last.then_inc(s_ht, 1)
                ready(dve, s_ht, b)
                v.tensor_scalar(be0[:, :], cnt[:, :], 1.0, None, ALU.max).then_inc(s_cntmax, 1)
                ready(dve, s_cntmax, b)
                v.reciprocal(be[:, :], be0[:, :]).then_inc(s_be, 1)

            def l0_zl(b):
                for m, ps in enumerate((A0, B0)):
                    dve.wait_ge(s_zh, b.number() * KN + m + 1)
                    last = low(zl[:, m, 0:F], ps[:, F:2 * F], zh[:, m, 0:F])
                last.then_inc(s_zl, 1)

            def l0_t(b):
                ready(dve, s_azmm, b)
                for m, ps in enumerate((A0, B0)):
                    last = v.tensor_scalar(deg[:, m:m + 1], ps[:, F:F + 1], EPS_DEG, None, ALU.max)
                last.then_inc(s_deg, 1)
                ready(dve, s_deg, b)
                v.reciprocal(rdeg[:, :], deg[:, :]).then_inc(s_rdeg, 1)
                ready(dve, s_rdeg, b)
                for m, ps in enumerate((A0, B0)):
                    last = v.scalar_tensor_tensor(t0[:, m, :], ps[:, 0:F], rdeg[:, m:m + 1], t0[:, m, :],
                                                  ALU.mult, ALU.add)
                last.then_inc(s_r0, 1)
                ready(dve, s_r0, b)
                s = b.slot(RING)
                dve.wait_ge(xm_in[s], b.dma_done(RING))
                v.scalar_tensor_tensor(t0[:, :, :], t0[:, :, :], 0.0,
                                       xm[:, s, 0:KN * F].rearrange("p (m f) -> p m f", f=F),
                                       ALU.max, ALU.add).then_inc(s_t0, 1)
                layer_norm(t0, bn0, mv0, rs0, x1, s_t0, s_bn0, s_mv0, s_rs0, s_x1, b)

            def l0_x1(b):
                reuse(dve, s_x1b, b)
                normalise(t0, mv0, rs0, x1, s_rs0, s_x1, b)

            def l0_x1l(b):
                ready(dve, s_x1h, b)
                low(x1l[:, :, :], x1[:, :, :], x1h[:, :, :]).then_inc(s_x1l, 1)

            def l0_dn(b):
                ready(dve, s_dnmm, b)
                ready(dve, s_azmm, b)
                v.tensor_reduce(dn[:, :], DN, AX.X, ALU.add).then_inc(s_dn, 1)
                ready(dve, s_dn, b)
                v.tensor_scalar(dpos[:, :], dn[:, :], 0.0, None, ALU.is_gt)
                v.tensor_scalar(dmax[:, :], dn[:, :], TINY, None, ALU.max).then_inc(s_dpos, 1)
                ready(dve, s_dpos, b)
                v.reciprocal(drec[:, :], dmax[:, :]).then_inc(s_drec, 1)
                ready(dve, s_drec, b)
                v.tensor_tensor(dnr[:, :], drec[:, :], dpos[:, :], ALU.mult).then_inc(s_dnr, 1)
                ready(dve, s_dnr, b)
                v.tensor_copy(dnb[:, :, :], dnr[:, :].unsqueeze(2).to_broadcast([P, KN, P])).then_inc(s_dnb, 1)

            def l0_hb(b):
                ready(dve, s_dntr, b)
                ready(dve, s_be, b)
                h = b.slot(2)
                for k in range(KN):
                    last = v.scalar_tensor_tensor(hb[:, k, :], f(ht[:, h, k, :]), be[:, k:k + 1], B0[:, 0:N],
                                                  ALU.mult, ALU.mult)
                last.then_inc(s_hb, 1)

            def l1_sl(b):
                ready(dve, s_sh, b)
                low(sl[:, :, :], tiles(A1), sh[:, :, :]).then_inc(s_sl, 1)

            def l1_sxl(b):
                ready(dve, s_sxh, b)
                low(sxl[:, :, :], tiles(B1), sxh[:, :, :]).then_inc(s_sxl, 1)

            def l1_r1l(b):
                for m in range(2):
                    dve.wait_ge(s_r1h2, b.number() * 2 + m + 1)
                    last = low(r1l[:, 2 * m:2 * m + 2, :], r1[:, 2 * m:2 * m + 2, :], r1h[:, 2 * m:2 * m + 2, :])
                last.then_inc(s_r1l, 1)

            def l1_hidden_var(b):
                ready(dve, s_vmm, b)
                for m, ps in enumerate((A1, B1)):
                    last = v.tensor_scalar(mu1[:, m:m + 1], ps[:, F:F + 1], 1.0 / H1, None, ALU.mult)
                last.then_inc(s_mu, 1)
                ready(dve, s_mu, b)
                v.tensor_tensor(mq1[:, :], mu1[:, :], mu1[:, :], ALU.mult).then_inc(s_mq, 1)
                ready(dve, s_mq, b)
                for m, ps in enumerate((A1, B1)):
                    last = v.scalar_tensor_tensor(var1[:, m:m + 1], ps[:, NO:NO + 1], 1.0 / H1, mq1[:, m:m + 1],
                                                  ALU.mult, ALU.subtract)
                last.then_inc(s_var, 1)
                ready(dve, s_var, b)
                v.tensor_scalar(vc1[:, :], var1[:, :], 0.0, None, ALU.max).then_inc(s_vc, 1)

            def l1_u(b):
                ready(dve, s_rsh, b)
                for m, ps in enumerate((A1, B1)):
                    last = v.scalar_tensor_tensor(u[:, m, :], ps[:, 0:F], rsh[:, m:m + 1], c2[:, :],
                                                  ALU.mult, ALU.add)
                last.then_inc(s_u, 1)

            def l1_ul(b):
                ready(dve, s_uh, b)
                low(ul[:, :, :], u[:, :, :], uh[:, :, :]).then_inc(s_ul, 1)

            def l1_t(b):
                ready(dve, s_ymm, b)
                ready(dve, s_x1b, b)
                v.scalar_tensor_tensor(t1[:, :, :], t1[:, :, :], 2.0, tiles(A1), ALU.mult, ALU.add).then_inc(s_t1, 1)
                layer_norm(t1, bn1, mv1, rs1, None, s_t1, s_bn1, s_mv1, s_rs1, s_x2, b)

            def l1_x2(b):
                normalise(t1, mv1, rs1, x2[:, b.slot(2), :, :], s_rs1, s_x2, b)

            def l1_x2ml(b):
                ready(dve, s_x2mh, b)
                for m in range(KN):
                    last = v.scalar_tensor_tensor(x2ml[:, m, :], x2[:, b.slot(2), m, :], mask_of(b, m),
                                                  f(x2mh[:, m, :]), ALU.mult, ALU.subtract)
                last.then_inc(s_x2ml, 1)

            def l2_x2tl(b):
                ready(dve, s_x2th, b)
                low(x2tl[:, :, :], tiles(A2), x2th[:, :, :]).then_inc(s_x2tl, 1)

            def l2_w(b):
                ready(dve, s_aggmm, b)
                ready(dve, s_qv, b)
                for m in range(KN):
                    last = v.scalar_tensor_tensor(qv[:, m, 0:F], tiles(B2)[:, m, :], mask_of(b, m), qv[:, m, 0:F],
                                                  ALU.mult, ALU.mult, accum_out=wdot[:, m:m + 1])
                last.then_inc(s_w2, 1)
                ready(dve, s_w2, b)
                v.tensor_copy(wb[:, :, :], wdot[:, :].unsqueeze(2).to_broadcast([P, KN, P])).then_inc(s_wb, 1)

            def l2_max(b):
                ready(dve, s_wtr, b)
                v.tensor_reduce(mx[:, :], A2[:, 0:N], AX.X, ALU.max).then_inc(s_mx, 1)
                ready(dve, s_mx, b)
                v.tensor_scalar(nmx[:, :], mx[:, :], -1.0, None, ALU.mult).then_inc(s_nmx, 1)

            def l2_t(b):
                ready(dve, s_esum, b)
                v.reciprocal(ercp[:, :], esum[:, :]).then_inc(s_ercp, 1)
                ready(dve, s_ercp, b)
                v.tensor_scalar(aw[:, :], ew[:, :], ercp[:, 0:1], None, ALU.mult).then_inc(s_a, 1)
                ready(dve, s_a, b)
                for m in range(KN):
                    last = v.scalar_tensor_tensor(t2[:, m, :], t2[:, m, :], aw[:, m:m + 1],
                                                  x2[:, b.slot(2), m, :], ALU.mult, ALU.add)
                last.then_inc(s_t2, 1)
                layer_norm(t2, bn2, mv2, rs2, None, s_t2, s_bn2, s_mv2, s_rs2, s_x3, b)

            def l2_x3(b):
                normalise(t2, mv2, rs2, x3[:, b.slot(2), :, :], s_rs2, s_x3, b)

            def l3_x3tl(b):
                ready(dve, s_x3th, b)
                low(x3tl[:, :, :], tiles(A3), x3th[:, :, :]).then_inc(s_x3tl, 1)

            def l3_y2l(b):
                ready(dve, s_y2h, b)
                reuse(dve, s_ez, b)
                for m, ps in enumerate((B3, A3)):
                    v.tensor_scalar(sj[:, m:m + 1], ps[:, F:F + 1], e_bias[:, 0:1], None, ALU.add)
                    last = v.tensor_copy(sib[:, m, :], ps[:, F + 1:F + 2].to_broadcast([P, P]))
                last.then_inc(s_sib, 1)
                for m, ps in enumerate((B3, A3)):
                    last = low(y2l[:, m, 0:F], ps[:, 0:F], y2h[:, m, 0:F])
                last.then_inc(s_y2l, 1)

            def l3_leaky(b):
                ready(dve, s_ez, b)
                v.scalar_tensor_tensor(al[:, :, :], al[:, :, :], SLOPE, al[:, :, :], ALU.mult, ALU.max).then_inc(s_el, 1)

            def l3_alpha(b):
                ready(dve, s_ee, b)
                v.tensor_tensor(al[:, :, :], al[:, :, :], at[:, b.slot(RING), :, :], ALU.mult).then_inc(s_al, 1)

            def l3_all(b):
                ready(dve, s_alh, b)
                low(all_[:, :, :], al[:, :, :], alh[:, :, :]).then_inc(s_all, 1)

            def l3_z3(b):
                ready(dve, s_p2mm, b)
                for m, ps in enumerate((A3, B3)):
                    last = v.tensor_scalar(rsum[:, m:m + 1], ps[:, F:F + 1], EPS_SUM, None, ALU.add)
                last.then_inc(s_rsum, 1)
                ready(dve, s_rsum, b)
                v.reciprocal(rrec[:, :], rsum[:, :]).then_inc(s_rrec, 1)
                ready(dve, s_rrec, b)
                for m, ps in enumerate((A3, B3)):
                    last = v.scalar_tensor_tensor(z3[:, m, :], ps[:, 0:F], rrec[:, m:m + 1], z3[:, m, :],
                                                  ALU.mult, ALU.add)
                last.then_inc(s_z3, 1)

            def l3_z3l(b):
                ready(dve, s_z3h, b)
                low(z3l[:, :, :], z3, z3h[:, :, :]).then_inc(s_z3l, 1)

            def l3_t(b):
                ready(dve, s_p1mm, b)
                ready(dve, s_y0b, b)
                for m in range(KN):
                    last = v.scalar_tensor_tensor(t3[:, m, :], tiles(A3)[:, m, :], rrec[:, m:m + 1], t3[:, m, :],
                                                  ALU.mult, ALU.add)
                last.then_inc(s_r3, 1)
                ready(dve, s_r3, b)
                v.scalar_tensor_tensor(t3, t3, 0.0, x3[:, b.slot(2), :, :],
                                       ALU.max, ALU.add).then_inc(s_t3, 1)
                layer_norm(t3, bn3, mv3, rs3, None, s_t3, s_bn3, s_mv3, s_rs3, s_xo, b)

            def l3_out(b):
                if not (isinstance(b.i, int) and b.c < 2):
                    dve.wait_ge(stored[b.slot(2)], b.dma_done(2) - 16)
                normalise(t3, mv3, rs3, xo[:, b.slot(2), :, :], s_rs3, s_xo, b)

            def step(of):
                bn, b0, b1, b2, b3 = of(-1), of(0), of(1), of(2), of(3)
                for stage, b in ((l0_h, b0), (l0_zl, b0), (l1_sl, b1), (l3_x3tl, b3), (l2_x2tl, b2),
                                 (l1_sxl, b1), (l3_y2l, b3), (l3_leaky, b3), (l3_alpha, b3), (l3_all, b3),
                                 (l2_w, b2), (l1_r1l, b1), (l2_max, b2), (l0_t, b0), (l2_t, b2), (l0_dn, b0),
                                 (l0_x1, b0), (l2_x3, b2), (l3_z3, b3), (l0_x1l, b0), (l3_z3l, b3),
                                 (l0_hb, b0), (l1_hidden_var, b1), (l0_split_x, bn), (l1_u, b1), (l1_ul, b1),
                                 (l3_t, b3), (l3_out, b3), (l1_t, b1), (l1_x2, b1), (l1_x2ml, b1)):
                    if b:
                        stage(b)

            constants()
            l0_split_x(Batch(0, 0))
            steps_of(dve, step)

        @block.gpsimd
        def _(pool):
            g = nc.gpsimd

            def l0_split_at(b):
                s = b.slot(RING)
                ready(pool, s_ath, b)
                g.tensor_tensor(atl[:, s, :, :], at[:, s, :, :], f(ath[:, s, :, :]), ALU.subtract).then_inc(s_atl, 1)
                ready(pool, s_atl, b)
                reuse(pool, s_dnmm, b)
                first, first_l = at[:, s, :, 0:1], f(atl[:, s, :, 0:1])
                g.tensor_tensor(wcol[:, :, 0:1], first, first_l, ALU.subtract)
                g.tensor_tensor(wcol[:, :, 1:2], first, f(ath[:, s, :, 0:1]), ALU.subtract).then_inc(s_wcol, 1)

            def l0_hbl(b):
                ready(pool, s_hbh, b)
                g.tensor_tensor(hbl[:, :, :], hb[:, :, :], f(hbh[:, :, :]), ALU.subtract).then_inc(s_hbl, 1)

            def l1_x1b(b):
                ready(pool, s_x1, b)
                reuse(pool, s_x2, b)
                g.tensor_tensor(t1[:, :, :], x1[:, :, :], b2_half[:, :].unsqueeze(1).to_broadcast([P, KN, F]), ALU.add).then_inc(s_x1b, 1)

            def l1_sq(b):
                for m in range(2):
                    pool.wait_ge(s_r1, b.number() * 2 + m + 1)
                    c = slice(2 * m, 2 * m + 2)
                    last = g.tensor_tensor(sq[:, c, :], r1[:, c, :], r1[:, c, :], ALU.mult)
                last.then_inc(s_sq, 1)
                ready(pool, s_sq, b)
                g.tensor_tensor(sq[:, 0:2, :], sq[:, 0:2, :], sq[:, 2:4, :], ALU.add).then_inc(s_sq2, 1)
                ready(pool, s_sq2, b)
                reuse(pool, s_vmm, b)
                g.tensor_tensor(sq1[:, :], sq[:, 0, :], sq[:, 1, :], ALU.add).then_inc(s_sq1, 1)

            def l3_y0b(b):
                ready(pool, s_y01, b)
                g.tensor_tensor(t3, t3, bk_sum[:, :].unsqueeze(1).to_broadcast([P, KN, F]), ALU.add).then_inc(s_y0b, 1)

            def step(of):
                b0, b1, b3 = of(0), of(1), of(3)
                for stage, b in ((l0_split_at, b0), (l1_x1b, b1), (l1_sq, b1), (l3_y0b, b3), (l0_hbl, b0)):
                    if b:
                        stage(b)

            pool.wait_ge(c_const, 1)
            steps_of(pool, step)


def kernel(x, adj, nodemask, L0_gnn_W, L1_gnn_W1, L1_gnn_b1, L1_gnn_gamma, L1_gnn_beta, L1_gnn_W2, L1_gnn_b2,
           L2_gnn_Wqk, L2_gnn_Wv, L3_gnn_Wv, L3_gnn_bv, L3_gnn_aw, L3_gnn_ab, L3_gnn_Wk, L3_gnn_bk):
    import numpy as np
    import concourse.bacc as bacc
    from concourse.bass_utils import run_bass_kernel_spmd

    def rows(a):
        a = np.asarray(a)
        k = a.shape[-2] // P
        a = a.reshape(a.shape[:-2] + (k, P, a.shape[-1]))
        return np.ascontiguousarray(np.moveaxis(a, -3, -2))

    def column(a):
        return np.ascontiguousarray(np.asarray(a).reshape(-1, P).T)

    x, adj, nodemask = np.asarray(x), np.asarray(adj), np.asarray(nodemask)
    W, Wk = np.asarray(L0_gnn_W).T, np.asarray(L3_gnn_Wk)
    aw = np.asarray(L3_gnn_aw)[:, 0].reshape(2, KF, P)
    arrays = {
        "at": rows(np.swapaxes(adj, 1, 2)),
        "xt": rows(np.swapaxes(x, 1, 2)),
        "xm": np.concatenate([rows(x).reshape(B, P, KN * F),
                              np.swapaxes(nodemask.reshape(B, KN, P), 1, 2)], axis=2),
        "w_l0": rows(np.concatenate([W[0:F], W[F:2 * F]], axis=1)),
        "w1": rows(np.asarray(L1_gnn_W1).T),
        "w2": rows(np.asarray(L1_gnn_W2).T),
        "wqk": rows(np.asarray(L2_gnn_Wqk).T),
        "wv2": rows(L2_gnn_Wv),
        "w3": rows(np.concatenate([Wk[0], Wk[1], Wk[2]], axis=1)),
        "wv3": rows(np.asarray(L3_gnn_Wv).T),
        "aw": np.ascontiguousarray(np.transpose(aw, (2, 1, 0))),
        "cols": np.concatenate([column(L1_gnn_b1), column(L1_gnn_gamma), column(L1_gnn_beta), column(L3_gnn_bv)], axis=1),
        "b2": np.ascontiguousarray(np.broadcast_to(np.asarray(L1_gnn_b2), (P, F))),
        "bk": np.ascontiguousarray(np.broadcast_to(np.asarray(L3_gnn_bk), (P, 3, F))),
        "ab": np.ascontiguousarray(np.broadcast_to(np.asarray(L3_gnn_ab), (P, 1))),
        "ident": np.eye(P, dtype=np.float32),
    }
    nc = bacc.Bacc("TRN2", target_bir_lowering=False, num_devices=1)
    arrays = {f"in_{k}": np.ascontiguousarray(a) for k, a in arrays.items()}
    args = [nc.dram_tensor(k, a.shape, mybir.dt.from_np(a.dtype), kind="ExternalInput").ap() for k, a in arrays.items()]
    args.append(nc.dram_tensor("out", (B, P, KN, F), F32, kind="ExternalOutput").ap())
    resnorm_kernel(nc, *args)
    r = run_bass_kernel_spmd(nc, [arrays], core_ids=[0])
    out = r.results[0]["out"]
    return np.ascontiguousarray(np.moveaxis(out, 2, 1).reshape(B, N, F))
```

```python
import concourse.bass as bass
from concourse import mybir
from contextlib import ExitStack

F32 = mybir.dt.float32
F32R = mybir.dt.float32r
ALU = mybir.AluOpType
ACT = mybir.ActivationFunctionType
AX = mybir.AxisListType

P = 128
B, N, F = 32, 256, 256
KN = N // P
KF = F // P
H1 = 512
KH = H1 // P
NO = N + 2
RING = 4
MIN_SKEW, MAX_SKEW = -2, 3
EPS_DEG, EPS_LN, EPS_SUM = 1e-6, 1e-5, 1e-12
TINY = 1.2e-38
SLOPE = 0.2



class Batch:

    def __init__(self, i, c):
        self.i, self.c = i, c
        self.is_first = isinstance(i, int) and c == 0

    def number(self):
        return self.i * RING + self.c

    def done(self):
        return self.i * RING + (self.c + 1)

    def slot(self, ring):
        return self.c % ring

    def dma_done(self, ring):
        return self.i * (16 * RING // ring) + 16 * (self.c // ring + 1)


def steps_of(eng, stages):
    def run(batch):
        for stage, skew in stages:
            b = batch(skew)
            if b:
                stage(b)

    head = MAX_SKEW + 1
    rounds = (B + MIN_SKEW - head) // RING
    for t in range(MIN_SKEW, head):
        run(lambda skew, t=t: Batch(0, t - skew) if t >= skew else None)
    with eng.Fori(0, rounds) as i:
        for u in range(RING):
            run(lambda skew, u=u: Batch(i, head + u - skew))
    for t in range(head + rounds * RING, B + MAX_SKEW):
        run(lambda skew, t=t: Batch(0, t - skew) if t - skew < B else None)


def resnorm_kernel(nc, at_d, xt_d, xm_d, w_l0_d, w1_d, w2_d, wqk_d, wv2_d, w3_d, wv3_d,
                   aw_d, cols_d, b2_d, bk_d, ab_d, ident_d, out_d):
    ctx = ExitStack()
    with ctx:
        def sb(name, shape, dt=F32):
            return ctx.enter_context(nc.sbuf_tensor(name, shape, dt))

        def sem(name):
            return ctx.enter_context(nc.semaphore(name))

        def sems(names):
            return [sem(n) for n in names.split()]

        ident = sb("ident", [P, P])
        ones = sb("ones", [P, P])
        eps_ln = sb("eps_ln", [P, 1])
        w3_raw = sb("w3_raw", [P, KF, 3 * F + 2])
        aw_raw = sb("aw_raw", [P, KF, 2])
        cols = sb("cols", [P, 14])
        b1c, gammac, betac, bvc = cols[:, 0:4], cols[:, 4:8], cols[:, 8:12], cols[:, 12:14]
        b2_half = sb("b2_half", [P, F])
        bk_sum = sb("bk_sum", [P, F])
        ab_b = sb("ab_b", [P, 1])
        c2 = sb("c2", [P, F])
        e_const = sb("e_const", [P, 2])
        e_bias = sb("e_bias", [P, 1])
        w0h, w0l = sb("w0h", [P, KF, 2 * F], F32R), sb("w0l", [P, KF, 2 * F], F32R)
        w1h, w1l = sb("w1h", [P, KF, H1], F32R), sb("w1l", [P, KF, H1], F32R)
        gh, gl = sb("gh", [P, KH, NO], F32R), sb("gl", [P, KH, NO], F32R)
        w2h, w2l = sb("w2h", [P, KF, 2 * F], F32R), sb("w2l", [P, KF, 2 * F], F32R)
        w3h, w3l = sb("w3h", [P, KF, 3 * F + 2], F32R), sb("w3l", [P, KF, 3 * F + 2], F32R)

        at = sb("at", [P, RING, KN, N])
        ath, atl = sb("ath", [P, RING, KN, N], F32R), sb("atl", [P, RING, KN, N], F32R)
        xt = sb("xt", [P, 2, KF, N])
        xm = sb("xm", [P, RING, KN * F + KN])

        x0th, x0tl = sb("x0th", [P, KF, N], F32R), sb("x0tl", [P, KF, N], F32R)
        t0 = sb("t0", [P, KN, F])
        zh, zl = sb("zh", [P, KN, NO], F32R), sb("zl", [P, KN, NO], F32R)
        deg, rdeg = sb("deg", [P, KN]), sb("rdeg", [P, KN])
        bn0, mv0, lv0, rs0 = sb("bn0", [P, KN, 6]), sb("mv0", [P, KN, 2]), sb("lv0", [P, KN]), sb("rs0", [P, KN])
        ht = sb("ht", [P, 2, KN, N], F32R)
        cnt, be0, be = sb("cnt", [P, KN]), sb("be0", [P, KN]), sb("be", [P, KN])
        wcol = sb("wcol", [P, KN, 2], F32R)
        dn, dpos, dmax, drec = sb("dn", [P, KN]), sb("dpos", [P, KN]), sb("dmax", [P, KN]), sb("drec", [P, KN])
        dnr = sb("dnr", [P, KN])
        dnb = sb("dnb", [P, KN, P])
        hb = sb("hb", [P, KN, N])
        hbh, hbl = sb("hbh", [P, KN, N], F32R), sb("hbl", [P, KN, N], F32R)
        x1 = sb("x1", [P, KN, F])
        nm0, nm2, nm3 = sb("nm0", [P, KN]), sb("nm2", [P, KN]), sb("nm3", [P, KN])
        x1h, x1l = sb("x1h", [P, KN, F], F32R), sb("x1l", [P, KN, F], F32R)

        sh, sl = sb("sh", [P, KN, N], F32R), sb("sl", [P, KN, N], F32R)
        sxh, sxl = sb("sxh", [P, KF, N], F32R), sb("sxl", [P, KF, N], F32R)
        r1 = sb("r1", [P, KH, N])
        r1h, r1l = sb("r1h", [P, KH, N], F32R), sb("r1l", [P, KH, N], F32R)
        sq = sb("sq", [P, KH, N])
        sq1 = sb("sq1", [P, N])
        mu1, mq1, var1, vc1 = sb("mu1", [P, KN]), sb("mq1", [P, KN]), sb("var1", [P, KN]), sb("vc1", [P, KN])
        lvh, rsh = sb("lvh", [P, KN]), sb("rsh", [P, KN])
        u = sb("u", [P, KN, F])
        uh, ul = sb("uh", [P, KN, F], F32R), sb("ul", [P, KN, F], F32R)
        t1 = sb("t1", [P, KN, F])
        bn1, mv1, lv1, rs1 = sb("bn1", [P, KN, 6]), sb("mv1", [P, KN, 2]), sb("lv1", [P, KN]), sb("rs1", [P, KN])
        x2 = sb("x2", [P, 2, KN, F])
        x2mh, x2ml = sb("x2mh", [P, KN, F], F32R), sb("x2ml", [P, KN, F], F32R)

        x2th, x2tl = sb("x2th", [P, KF, N], F32R), sb("x2tl", [P, KF, N], F32R)
        qv = sb("qv", [P, KN, 2 * F])
        wdot = sb("wdot", [P, KN])
        wb = sb("wb", [P, KN, P])
        mx, nmx = sb("mx", [P, 1]), sb("nmx", [P, 1])
        ejunk, esum, ercp = sb("ejunk", [P, N]), sb("esum", [P, 1]), sb("ercp", [P, 1])
        ew, aw = sb("ew", [P, KN]), sb("aw", [P, KN])
        t2 = qv[:, :, F:2 * F]
        bn2, mv2, lv2, rs2 = sb("bn2", [P, KN, 6]), sb("mv2", [P, KN, 2]), sb("lv2", [P, KN]), sb("rs2", [P, KN])
        x3 = sb("x3", [P, 2, KN, F])

        x3th, x3tl = sb("x3th", [P, KF, N], F32R), sb("x3tl", [P, KF, N], F32R)
        y2h, y2l = sb("y2h", [P, KN, NO], F32R), sb("y2l", [P, KN, NO], F32R)
        sj = sb("sj", [P, KN])
        sib = sb("sib", [P, KN, P])
        y01 = sb("y01", [P, KN, 2 * F])
        t3 = y01[:, :, 0:F]
        z3 = y01[:, :, F:2 * F]
        al = sb("al", [P, KN, N])
        alh, all_ = sb("alh", [P, KN, N], F32R), sb("all", [P, KN, N], F32R)
        rsum, rrec = sb("rsum", [P, KN]), sb("rrec", [P, KN])
        z3h, z3l = sb("z3h", [P, KN, F], F32R), sb("z3l", [P, KN, F], F32R)
        bn3, mv3, lv3, rs3 = sb("bn3", [P, KN, 6]), sb("mv3", [P, KN, 2]), sb("lv3", [P, KN]), sb("rs3", [P, KN])
        xo = sb("xo", [P, 2, KN, F])

        def over(tile, k):
            return tile.rearrange("p a b -> p (a b)").rearrange("p (k f) -> p k f", k=k)

        w0_raw, w1_raw = over(x3[:, 0:2, :, :].rearrange("p a b c -> p a (b c)"), KF), over(xo[:, 0:2, :, :].rearrange("p a b c -> p a (b c)"), KF)
        w2_raw, g_raw, wqk_raw, l2_raw = r1[:, :, :], sq[:, :, :], over(qv[:, :, :], KH), y01[:, :, :]
        wv3_raw, beta_b, bv_b = t1[:, :, :], over(u[:, :, :], KH), al[:, :, 0:P]
        bk_raw = over(x2[:, 0:2, :, :].rearrange("p a b c -> p a (b c)"), KH)[:, 0:3, :]
        g_mean = x1[:, 0, :]

        bank = [ctx.enter_context(nc.psum_tensor(f"bank{i}", [P, 512], F32)) for i in range(8)]
        A0, B0, A1, B1, A2, B2, A3, B3 = bank
        DN = A0[:, 264:264 + 2 * KN].rearrange("p (m c) -> p m c", c=2)

        def tiles(ps, n=KN, w=F):
            return ps[:, 0:n * w].rearrange("p (m f) -> p m f", f=w)

        def f(ap):
            return ap.bitcast(F32)

        s_w = sem("weights_loaded")
        s_memset = sem("constants_set")
        c_m, c_mean, c_c2, c_u, c_e = sems("c_m c_mean c_c2 c_u c_e")
        c_g, c_bcast, c_gc, c_l2, c_u3, c_const, c_dve, c_wready, c_act = sems(
            "c_g c_bcast c_gc c_l2 c_u3 c_const c_dve c_wready c_act")
        at_in = [sem(f"at_in{i}") for i in range(RING)]
        xt_in = [sem(f"xt_in{i}") for i in range(2)]
        xm_in = [sem(f"xm_in{i}") for i in range(RING)]
        stored = [sem(f"stored{i}") for i in range(2)]
        s_x0th, s_x0tl, s_ath, s_atl, s_ht, s_cntmax, s_be, s_wcol = sems(
            "x0th_ready x0tl_ready ath_ready atl_ready ht_ready count_clamped be_ready wcol_ready")
        s_y0mm, s_zh, s_zl, s_azmm, s_deg, s_rdeg, s_r0, s_t0 = sems(
            "y0_done zh_ready zl_ready az_done deg_ready rdeg_ready r0_ready t0_ready")
        s_bn0, s_mv0, s_lv0, s_rs0, s_x1, s_x1h, s_x1l = sems(
            "bn0_ready mv0_ready lv0_ready rs0_ready x1_ready x1h_ready x1l_ready")
        s_dnmm, s_dn, s_dpos, s_drec, s_dnr, s_dnb, s_dntr, s_hb, s_hbh, s_hbl = sems(
            "dn_done dn_ready dpos_ready drec_ready dnr_ready dnb_ready dnb_transposed hb_ready hbh_ready hbl_ready")
        s_smm, s_sh, s_sl, s_sxmm, s_sxh, s_sxl, s_rmm, s_r1, s_r1h, s_r1l = sems(
            "s_done sh_ready sl_ready sx_done sxh_ready sxl_ready r_done r1_ready r1h_ready r1l_ready")
        s_sq, s_sq2, s_sq1, s_vmm, s_mu, s_mq, s_var, s_vc, s_lvh, s_rsh = sems(
            "sq_ready sq2_ready sq1_ready v_done mu_ready mq_ready var_ready varc_ready lvh_ready rsh_ready")
        s_u, s_uh, s_ul, s_x1b, s_ymm, s_t1, s_bn1, s_mv1, s_lv1, s_rs1, s_x2, s_x2mh, s_x2ml = sems(
            "u_ready uh_ready ul_ready x1b_ready y_done t1_ready bn1_ready mv1_ready lv1_ready rs1_ready "
            "x2_ready x2mh_ready x2ml_ready")
        s_x2tr, s_x2th, s_x2tl, s_qvmm, s_qv, s_aggmm, s_w2, s_wb, s_wtr, s_mx, s_nmx, s_esum, s_ercp, s_a = sems(
            "x2_transposed x2th_ready x2tl_ready qv_done qv_ready agg_done w_ready wb_ready w_transposed "
            "max_ready negmax_ready exps_ready ercp_ready a_ready")
        s_t2, s_bn2, s_mv2, s_lv2, s_rs2, s_x3 = sems("t2_ready bn2_ready mv2_ready lv2_ready rs2_ready x3_ready")
        s_x3tr, s_x3th, s_x3tl, s_y2mm, s_y2h, s_y2l, s_sib, s_sitr, s_ez, s_el, s_ee, s_al, s_alh, s_all = sems(
            "x3_transposed x3th_ready x3tl_ready y2_done y2h_ready y2l_ready sib_ready si_transposed "
            "ez_ready el_ready ee_ready alpha_ready alh_ready all_ready")
        s_y01mm, s_y01, s_y0b, s_p2mm, s_rsum, s_rrec, s_z3, s_z3h, s_z3l, s_p1mm, s_r3, s_t3 = sems(
            "y01_done y01_ready y0b_ready p2_done rowsum_ready rrec_ready z3_ready z3h_ready z3l_ready "
            "p1_done r3_ready t3_ready")
        s_bn3, s_mv3, s_lv3, s_rs3, s_xo = sems("bn3_ready mv3_ready lv3_ready rs3_ready out_ready")

        s_nm0, s_nm2, s_nm3 = sems("nm0_ready nm2_ready nm3_ready")
        s_r1h2, s_r1l2 = sems("r1h_half_ready r1l_first_half_ready")

        def mask_of(b, m):
            return xm[:, b.slot(RING), KN * F + m:KN * F + m + 1]

        def ready(eng, s, b):
            eng.wait_ge(s, b.done())

        def reuse(eng, s, b):
            if not b.is_first:
                eng.wait_ge(s, b.number())

        block = ctx.enter_context(nc.Block())

        n_weights = 13

        @block.sync
        def _(sp):
            def load_at(b):
                sp.dma_start(at[:, b.slot(RING), :, :], at_d[b.number(), :, :, :]).then_inc(at_in[b.slot(RING)], 16)

            def load_xt(b):
                sp.dma_start(xt[:, b.slot(2), :, :], xt_d[b.number(), :, :, :]).then_inc(xt_in[b.slot(2)], 16)

            def load_xm(b):
                sp.dma_start(xm[:, b.slot(RING), :], xm_d[b.number(), :, :]).then_inc(xm_in[b.slot(RING)], 16)

            for dst, src in ((w0_raw, w_l0_d), (cols[:, :], cols_d), (w1_raw, w1_d), (w2_raw, w2_d),
                             (ident[:, :], ident_d), (wqk_raw, wqk_d),
                             (l2_raw[:, :, F:2 * F], wv2_d), (w3_raw[:, :, 0:3 * F], w3_d),
                             (wv3_raw, wv3_d), (aw_raw[:, :, :], aw_d), (b2_half[:, :], b2_d),
                             (bk_raw, bk_d), (ab_b[:, :], ab_d)):
                sp.dma_start(dst, src).then_inc(s_w, 16)

            def load_x(b):
                if not (isinstance(b.i, int) and b.c < 2):
                    sp.wait_ge(s_x0tl, b.number() - 1)
                load_xt(b)
                if not (isinstance(b.i, int) and b.c < RING):
                    sp.wait_ge(s_w2, b.number() - (RING - 1))
                    sp.wait_ge(s_x2ml, b.number() - (RING - 1))
                load_xm(b)

            def load_adj(b):
                if not (isinstance(b.i, int) and b.c < RING):
                    sp.wait_ge(s_al, b.number() - (RING - 1))
                load_at(b)

            def store(b):
                ready(sp, s_xo, b)
                sp.dma_start(out_d[b.number(), :, :, :], xo[:, b.slot(2), :, :]).then_inc(stored[b.slot(2)], 16)

            steps_of(sp, [(load_x, -2), (load_adj, -2), (store, 3)])
            for s in stored:
                sp.wait_ge(s, 16 * B // 2)

        @block.tensor
        def _(pe):
            def mm(out, lhs, rhs, start, stop):
                return nc.tensor.matmul(out, lhs, rhs, start=start, stop=stop)

            def product(out, lhs, rhs, k_tiles):
                for k in range(k_tiles):
                    (lh, ll), (rh, rl) = lhs(k), rhs(k)
                    mm(out, lh, rh, k == 0, False)
                    mm(out, lh, rl, False, False)
                    last = mm(out, ll, rh, False, k == k_tiles - 1)
                return last

            def cut(m):
                return slice(m * P, (m + 1) * P)

            def transposes(ps, src):
                for m in range(KN):
                    for k in range(KF):
                        last = nc.tensor.transpose(tiles(ps)[:, k, cut(m)], src[:, m, cut(k)], ident[:, :])
                return last

            def constants():
                pe.wait_ge(s_w, 16 * n_weights)
                for m in range(KF):
                    for k in range(KF):
                        last = mm(tiles(A2)[:, m, :], wqk_raw[:, k, cut(m)], wqk_raw[:, KF + k, :], k == 0, k == KF - 1)
                last.then_inc(c_m, 1)
                pe.wait_ge(c_g, 1)
                pe.wait_ge(s_memset, 1)
                for k in range(KH):
                    last = mm(A1[:, 0:F], ones[:, :], g_raw[:, k, :], k == 0, k == KH - 1)
                last.then_inc(c_mean, 1)
                pe.wait_ge(c_bcast, 1)
                for k in range(KH):
                    last = mm(B1[:, 0:F], beta_b[:, k, :], w2_raw[:, k, :], k == 0, k == KH - 1)
                last.then_inc(c_c2, 1)
                for m in range(KF):
                    for k in range(KF):
                        last = mm(A3[:, 2 * m:2 * m + 2], wv3_raw[:, k, cut(m)], aw_raw[:, k, :], k == 0, k == KF - 1)
                last.then_inc(c_u, 1)
                for k in range(KF):
                    last = mm(B3[:, 0:2], bv_b[:, k, :], aw_raw[:, k, :], k == 0, k == KF - 1)
                last.then_inc(c_e, 1)

            def l0_y(b):
                ready(pe, s_x0tl, b)
                ready(pe, s_x0th, b)
                reuse(pe, s_r0, b)
                reuse(pe, s_hb, b)
                for m, ps in enumerate((A0, B0)):
                    last = product(ps[:, :], lambda k: (x0th[:, k, cut(m)], x0tl[:, k, cut(m)]),
                                   lambda k: (w0h[:, k, :], w0l[:, k, :]), KF)
                    last.then_inc(s_y0mm, 1)

            def l0_az(b):
                s = b.slot(RING)
                ready(pe, s_zl, b)
                ready(pe, s_atl, b)
                ready(pe, s_ath, b)
                for m, ps in enumerate((A0, B0)):
                    last = product(ps[:, 0:NO], lambda k: (ath[:, s, k, cut(m)], atl[:, s, k, cut(m)]),
                                   lambda k: (zh[:, k, :], zl[:, k, :]), KN)
                last.then_inc(s_azmm, 1)

            def l0_dn(b):
                h = b.slot(2)
                ready(pe, s_zl, b)
                ready(pe, s_ht, b)
                ready(pe, s_wcol, b)
                for m in range(KN):
                    for k in range(KN):
                        last = mm(DN[:, m, :], ht[:, h, k, cut(m)], wcol[:, k, :], k == 0, k == KN - 1)
                last.then_inc(s_dnmm, 1)

            def l0_dn_rows(b):
                ready(pe, s_dnb, b)
                ready(pe, s_r0, b)
                for m in range(KN):
                    last = nc.tensor.transpose(B0[:, cut(m)], dnb[:, m, :], ident[:, :])
                last.then_inc(s_dntr, 1)

            def l1_s(b):
                h = b.slot(2)
                ready(pe, s_hbl, b)
                ready(pe, s_hbh, b)
                ready(pe, s_ht, b)
                reuse(pe, s_t1, b)
                for m in range(KN):
                    for k in range(KN):
                        mm(tiles(A1)[:, m, :], ht[:, h, k, cut(m)], hbh[:, k, :], k == 0, False)
                        last = mm(tiles(A1)[:, m, :], ht[:, h, k, cut(m)], hbl[:, k, :], False, k == KN - 1)
                last.then_inc(s_smm, 1)

            def l1_sx(b):
                ready(pe, s_sl, b)
                ready(pe, s_sh, b)
                ready(pe, s_x1l, b)
                ready(pe, s_x1h, b)
                reuse(pe, s_u, b)
                for m in range(KF):
                    last = product(tiles(B1)[:, m, :], lambda k: (x1h[:, k, cut(m)], x1l[:, k, cut(m)]),
                                   lambda k: (sh[:, k, :], sl[:, k, :]), KN)
                last.then_inc(s_sxmm, 1)

            def l1_r(b):
                ready(pe, s_sxl, b)
                ready(pe, s_sxh, b)
                for m in range(KH):
                    last = product(tiles((A1, B1)[m // 2])[:, m % 2, :],
                                   lambda k: (w1h[:, k, cut(m)], w1l[:, k, cut(m)]),
                                   lambda k: (sxh[:, k, :], sxl[:, k, :]), KF)
                    if m % 2:
                        last.then_inc(s_rmm, 1)

            def l1_v(b):
                ready(pe, s_r1l2, b)
                ready(pe, s_r1l, b)
                for m, ps in enumerate((A1, B1)):
                    product(ps[:, 0:NO], lambda k: (r1h[:, k, cut(m)], r1l[:, k, cut(m)]),
                            lambda k: (gh[:, k, :], gl[:, k, :]), KH)
                ready(pe, s_sq1, b)
                for m, ps in enumerate((A1, B1)):
                    last = mm(ps[:, NO:NO + 1], sq1[:, cut(m)], ones[:, 0:1], True, True)
                last.then_inc(s_vmm, 1)

            def l1_y(b):
                ready(pe, s_ul, b)
                ready(pe, s_uh, b)
                for m in range(KN):
                    last = product(tiles(A1)[:, m, :], lambda k: (sh[:, k, cut(m)], sl[:, k, cut(m)]),
                                   lambda k: (uh[:, k, :], ul[:, k, :]), KN)
                last.then_inc(s_ymm, 1)

            def l2_tr(b):
                ready(pe, s_x2, b)
                reuse(pe, s_esum, b)
                transposes(A2, x2[:, b.slot(2), :, :]).then_inc(s_x2tr, 1)

            def l2_qv(b):
                ready(pe, s_x2tl, b)
                ready(pe, s_x2th, b)
                reuse(pe, s_w2, b)
                for m, ps in enumerate((B2, A2)):
                    last = product(ps[:, :], lambda k: (x2th[:, k, cut(m)], x2tl[:, k, cut(m)]),
                                   lambda k: (w2h[:, k, :], w2l[:, k, :]), KF)
                    last.then_inc(s_qvmm, 1)

            def l2_agg(b):
                s = b.slot(RING)
                ready(pe, s_x2ml, b)
                ready(pe, s_x2mh, b)
                ready(pe, s_qv, b)
                for m in range(KN):
                    last = product(tiles(B2)[:, m, :], lambda k: (ath[:, s, k, cut(m)], atl[:, s, k, cut(m)]),
                                   lambda k: (x2mh[:, k, :], x2ml[:, k, :]), KN)
                last.then_inc(s_aggmm, 1)

            def l2_w_rows(b):
                ready(pe, s_wb, b)
                for m in range(KN):
                    last = nc.tensor.transpose(A2[:, cut(m)], wb[:, m, :], ident[:, :])
                last.then_inc(s_wtr, 1)

            def l3_tr(b):
                ready(pe, s_x3, b)
                reuse(pe, s_r3, b)
                transposes(A3, x3[:, b.slot(2), :, :]).then_inc(s_x3tr, 1)

            def l3_y2(b):
                ready(pe, s_x3tl, b)
                ready(pe, s_x3th, b)
                reuse(pe, s_z3, b)
                for m, ps in enumerate((B3, A3)):
                    last = product(ps[:, 0:NO], lambda k: (x3th[:, k, cut(m)], x3tl[:, k, cut(m)]),
                                   lambda k: (w3h[:, k, 2 * F:3 * F + 2], w3l[:, k, 2 * F:3 * F + 2]), KF)
                    last.then_inc(s_y2mm, 1)

            def l3_si_rows(b):
                ready(pe, s_sib, b)
                ready(pe, s_y2l, b)
                for m in range(KN):
                    last = nc.tensor.transpose(B3[:, cut(m)], sib[:, m, :], ident[:, :])
                last.then_inc(s_sitr, 1)

            def l3_y01(b):
                ready(pe, s_y2l, b)
                ready(pe, s_ez, b)
                for m, ps in enumerate((A3, B3)):
                    last = product(ps[:, :], lambda k: (x3th[:, k, cut(m)], x3tl[:, k, cut(m)]),
                                   lambda k: (w3h[:, k, 0:2 * F], w3l[:, k, 0:2 * F]), KF)
                    last.then_inc(s_y01mm, 1)

            def l3_p2(b):
                ready(pe, s_all, b)
                ready(pe, s_alh, b)
                ready(pe, s_y2h, b)
                ready(pe, s_y01, b)
                for m, ps in enumerate((A3, B3)):
                    last = product(ps[:, 0:NO], lambda k: (alh[:, k, cut(m)], all_[:, k, cut(m)]),
                                   lambda k: (y2h[:, k, :], y2l[:, k, :]), KN)
                last.then_inc(s_p2mm, 1)

            def l3_p1(b):
                ready(pe, s_z3l, b)
                ready(pe, s_z3h, b)
                for m in range(KN):
                    last = product(tiles(A3)[:, m, :], lambda k: (alh[:, k, cut(m)], all_[:, k, cut(m)]),
                                   lambda k: (z3h[:, k, :], z3l[:, k, :]), KN)
                last.then_inc(s_p1mm, 1)

            stages = [
                (l3_y01, 3), (l1_v, 1), (l2_agg, 2), (l3_p2, 3), (l2_w_rows, 2), (l0_y, -1), (l1_y, 1),
                (l3_p1, 3), (l1_s, 0), (l0_az, -1), (l3_tr, 2), (l1_sx, 0), (l0_dn, -1), (l3_y2, 2), (l2_tr, 1),
                (l1_r, 0), (l3_si_rows, 2), (l2_qv, 1), (l0_dn_rows, -1),
            ]

            pe.wait_ge(c_wready, 1)
            constants()
            pe.wait_ge(c_const, 1)
            steps_of(pe, stages)

        @block.scalar
        def _(act):
            def copy(out, src, **kw):
                return nc.scalar.activation(out, src, ACT.Identity, **kw)

            def rstd(lv, rs, mv, s_mv, s_lv, s_rs, b):
                ready(act, s_mv, b)
                nc.scalar.activation(lv[:, :], mv, ACT.Ln, bias=eps_ln[:, 0:1]).then_inc(s_lv, 1)
                ready(act, s_lv, b)
                nc.scalar.activation(rs[:, :], lv[:, :], ACT.Exp, scale=-0.5).then_inc(s_rs, 1)

            def normalise(t, rs, nm, out, s_nm, s_out, b):
                ready(act, s_nm, b)
                for m in range(KN):
                    last = copy(out[:, m, :], t[:, m, :], bias=nm[:, m:m + 1], scale=rs[:, m:m + 1])
                last.then_inc(s_out, 1)

            def constants():
                act.wait_ge(s_w, 16 * n_weights)
                copy(w0h[:, :, :], w0_raw)
                copy(w1h[:, :, :], w1_raw).then_inc(c_act, 1)
                act.wait_ge(c_gc, 1)
                copy(gh[:, :, 0:F], g_raw[:, :, :]).then_inc(c_act, 1)
                act.wait_ge(c_l2, 1)
                copy(w2h[:, :, :], l2_raw[:, :, :]).then_inc(c_act, 1)
                act.wait_ge(c_u3, 1)
                copy(w3h[:, :, :], w3_raw[:, :, :]).then_inc(c_act, 1)

            def l0_split_x(b):
                act.wait_ge(xt_in[b.slot(2)], b.dma_done(2))
                reuse_c = Batch(b.i, b.c)
                if not reuse_c.is_first:
                    act.wait_ge(s_y0mm, b.number() * KN)
                copy(x0th[:, :, :], xt[:, b.slot(2), :, :]).then_inc(s_x0th, 1)

            def l0_split_at(b):
                s = b.slot(RING)
                act.wait_ge(at_in[s], b.dma_done(RING))
                copy(ath[:, s, :, :], at[:, s, :, :]).then_inc(s_ath, 1)

            def l0_z(b):
                for m, ps in enumerate((A0, B0)):
                    act.wait_ge(s_y0mm, b.number() * KN + m + 1)
                    if m == 0:
                        reuse(act, s_azmm, b)
                        reuse(act, s_x1, b)
                    copy(zh[:, m, 0:F], ps[:, F:2 * F])
                    copy(t0[:, m, :], ps[:, 0:F]).then_inc(s_zh, 1)

            def l0_rstd(b):
                rstd(lv0, rs0, mv0[:, :, 1], s_mv0, s_lv0, s_rs0, b)

            def l0_x1(b):
                reuse(act, s_x1b, b)
                reuse(act, s_x1l, b)
                normalise(t0, rs0, nm0, x1, s_nm0, s_x1, b)

            def l0_x1h(b):
                ready(act, s_x1, b)
                reuse(act, s_sxmm, b)
                copy(x1h[:, :, :], x1[:, :, :]).then_inc(s_x1h, 1)

            def l0_hbh(b):
                ready(act, s_hb, b)
                reuse(act, s_smm, b)
                copy(hbh[:, :, :], hb[:, :, :]).then_inc(s_hbh, 1)

            def l1_sh(b):
                ready(act, s_smm, b)
                reuse(act, s_ymm, b)
                copy(sh[:, :, :], tiles(A1)).then_inc(s_sh, 1)

            def l1_sxh(b):
                ready(act, s_sxmm, b)
                act.wait_ge(s_rmm, b.number() * 2) if not b.is_first else None
                copy(sxh[:, :, :], tiles(B1)).then_inc(s_sxh, 1)

            def l1_r1(b):
                reuse(act, s_r1l, b)
                reuse(act, s_r1l2, b)
                for m in range(KH):
                    if m % 2 == 0:
                        act.wait_ge(s_rmm, b.number() * 2 + m // 2 + 1)
                    last = nc.scalar.activation(r1[:, m, :], tiles((A1, B1)[m // 2])[:, m % 2, :], ACT.Relu,
                                                bias=b1c[:, m:m + 1])
                    if m % 2:
                        last.then_inc(s_r1, 1)

            def l1_sq(b):
                reuse(act, s_sq1, b)
                for m in range(2):
                    act.wait_ge(s_r1, b.number() * 2 + m + 1)
                    c = slice(2 * m, 2 * m + 2)
                    last = nc.scalar.activation(sq[:, c, :], r1[:, c, :], ACT.Square)
                last.then_inc(s_sq, 1)

            def l1_r1h(b):
                reuse(act, s_vmm, b)
                for m in range(2):
                    act.wait_ge(s_r1, b.number() * 2 + m + 1)
                    copy(r1h[:, 2 * m:2 * m + 2, :], r1[:, 2 * m:2 * m + 2, :]).then_inc(s_r1h2, 1)

            def l1_hidden_rstd(b):
                rstd(lvh, rsh, vc1[:, :], s_vc, s_lvh, s_rsh, b)

            def l1_uh(b):
                ready(act, s_u, b)
                reuse(act, s_ymm, b)
                copy(uh[:, :, :], u[:, :, :]).then_inc(s_uh, 1)

            def l1_rstd(b):
                rstd(lv1, rs1, mv1[:, :, 1], s_mv1, s_lv1, s_rs1, b)

            def l1_x2mh(b):
                ready(act, s_x2, b)
                reuse(act, s_aggmm, b)
                for m in range(KN):
                    last = copy(x2mh[:, m, :], x2[:, b.slot(2), m, :], scale=mask_of(b, m))
                last.then_inc(s_x2mh, 1)

            def l2_x2th(b):
                ready(act, s_x2tr, b)
                if not b.is_first:
                    act.wait_ge(s_qvmm, b.number() * KN)
                copy(x2th[:, :, :], tiles(A2)).then_inc(s_x2th, 1)

            def l2_qv(b):
                reuse(act, s_x3, b)
                for m, ps in enumerate((B2, A2)):
                    act.wait_ge(s_qvmm, b.number() * KN + m + 1)
                    last = copy(qv[:, m, :], ps[:, :])
                last.then_inc(s_qv, 1)

            def l2_exp(b):
                ready(act, s_nmx, b)
                nc.scalar.activation(ew[:, :], wdot[:, :], ACT.Exp, bias=nmx[:, 0:1])
                nc.scalar.activation(ejunk[:, :], A2[:, 0:N], ACT.Exp, bias=nmx[:, 0:1],
                                     accum_out=esum[:, 0:1]).then_inc(s_esum, 1)

            def l2_rstd(b):
                rstd(lv2, rs2, mv2[:, :, 1], s_mv2, s_lv2, s_rs2, b)

            def l2_x3(b):
                normalise(t2, rs2, nm2, x3[:, b.slot(2), :, :], s_nm2, s_x3, b)

            def l3_x3th(b):
                ready(act, s_x3tr, b)
                if not b.is_first:
                    act.wait_ge(s_y01mm, b.number() * KN)
                copy(x3th[:, :, :], tiles(A3)).then_inc(s_x3th, 1)

            def l3_y2h(b):
                reuse(act, s_p2mm, b)
                for m, ps in enumerate((B3, A3)):
                    act.wait_ge(s_y2mm, b.number() * KN + m + 1)
                    last = copy(y2h[:, m, 0:F], ps[:, 0:F])
                last.then_inc(s_y2h, 1)

            def l3_ez(b):
                ready(act, s_sitr, b)
                reuse(act, s_all, b)
                for m in range(KN):
                    last = copy(al[:, m, :], B3[:, 0:N], bias=sj[:, m:m + 1])
                last.then_inc(s_ez, 1)

            def l3_exp(b):
                ready(act, s_el, b)
                nc.scalar.activation(al[:, :, :], al[:, :, :], ACT.Exp).then_inc(s_ee, 1)

            def l3_alh(b):
                ready(act, s_al, b)
                reuse(act, s_p1mm, b)
                copy(alh[:, :, :], al[:, :, :]).then_inc(s_alh, 1)

            def l3_y01(b):
                reuse(act, s_z3l, b)
                reuse(act, s_xo, b)
                for m, ps in enumerate((A3, B3)):
                    act.wait_ge(s_y01mm, b.number() * KN + m + 1)
                    last = copy(y01[:, m, :], ps[:, :])
                last.then_inc(s_y01, 1)

            def l3_z3h(b):
                ready(act, s_z3, b)
                reuse(act, s_p1mm, b)
                copy(z3h[:, :, :], z3).then_inc(s_z3h, 1)

            def l3_rstd(b):
                rstd(lv3, rs3, mv3[:, :, 1], s_mv3, s_lv3, s_rs3, b)

            def l3_out(b):
                if not (isinstance(b.i, int) and b.c < 2):
                    act.wait_ge(stored[b.slot(2)], b.dma_done(2) - 16)
                normalise(t3, rs3, nm3, xo[:, b.slot(2), :, :], s_nm3, s_xo, b)

            stages = [
                (l3_exp, 3), (l1_sq, 1), (l2_qv, 2), (l0_split_x, -1), (l3_alh, 3), (l3_y01, 3), (l0_rstd, 0),
                (l0_hbh, 0), (l0_split_at, -1), (l1_hidden_rstd, 1), (l0_x1, 0), (l1_uh, 1), (l2_exp, 2),
                (l3_z3h, 3), (l0_z, -1), (l0_x1h, 0), (l2_rstd, 2), (l2_x3, 2), (l1_sh, 0), (l3_x3th, 2),
                (l1_rstd, 1), (l1_sxh, 0), (l3_y2h, 2), (l2_x2th, 1), (l1_x2mh, 1), (l3_rstd, 3), (l1_r1, 0),
                (l3_ez, 2), (l1_r1h, 0), (l3_out, 3),
            ]

            nc.scalar.preload_act_table_set("natural_log_exp_and_others")
            constants()
            steps_of(act, stages)

        @block.vector
        def _(dve):
            v = nc.vector

            def row_stats(t, bn, mv, s_t, s_bn, s_mv, b):
                ready(dve, s_t, b)
                for m in range(KN):
                    last = v.bn_stats(bn[:, m, :], t[:, m, :])
                last.then_inc(s_bn, 1)
                dve.wait_ge(s_memset, 1)
                ready(dve, s_bn, b)
                for m in range(KN):
                    last = v.bn_aggr(mv[:, m, :], bn[:, m, :])
                last.then_inc(s_mv, 1)

            def shift(mv, rs, nm, s_rs, s_nm, b):
                ready(dve, s_rs, b)
                v.scalar_tensor_tensor(nm[:, :], mv[:, :, 0], -1.0, rs[:, :], ALU.mult, ALU.mult).then_inc(s_nm, 1)

            def normalise(t, mv, rs, out, s_rs, s_out, b):
                ready(dve, s_rs, b)
                for m in range(KN):
                    last = v.tensor_scalar(out[:, m, :], t[:, m, :], mv[:, m, 0:1], rs[:, m:m + 1],
                                           ALU.subtract, ALU.mult)
                last.then_inc(s_out, 1)

            def low(out, whole, high):
                return v.tensor_tensor(out, whole, f(high), ALU.subtract)

            def constants():
                v.memset(ones[:, :], 1.0)
                v.memset(eps_ln[:, :], EPS_LN).then_inc(s_memset, 1)
                for t, val in ((zh, 1.0), (zl, 0.0), (y2h, 1.0), (y2l, 0.0), (gh, 1.0), (gl, 0.0)):
                    v.memset(f(t[:, :, F:NO]), val)
                dve.wait_ge(s_w, 16 * n_weights)
                for k in range(KH):
                    last = v.tensor_scalar(g_raw[:, k, :], w2_raw[:, k, :], gammac[:, k:k + 1], None, ALU.mult)
                last.then_inc(c_g, 1)
                dve.wait_ge(s_memset, 1)
                for k in range(KH):
                    v.tensor_scalar(beta_b[:, k, :], ones[:, :], betac[:, k:k + 1], None, ALU.mult)
                for k in range(KF):
                    last = v.tensor_scalar(bv_b[:, k, :], ones[:, :], bvc[:, k:k + 1], None, ALU.mult)
                last.then_inc(c_bcast, 1)
                dve.wait_ge(c_act, 1)
                low(w0l[:, :, :], w0_raw, w0h[:, :, :]).then_inc(c_wready, 1)
                low(w1l[:, :, :], w1_raw, w1h[:, :, :])
                dve.wait_ge(c_m, 1)
                v.tensor_scalar(l2_raw[:, :, 0:F], tiles(A2), float(F) ** -0.5, None, ALU.mult).then_inc(c_l2, 1)
                dve.wait_ge(c_mean, 1)
                v.tensor_scalar(g_mean, A1[:, 0:F], 1.0 / H1, None, ALU.mult).then_inc(c_dve, 1)
                dve.wait_ge(c_dve, 1)
                dve.wait_ge(c_g, 1)
                for k in range(KH):
                    last = v.tensor_tensor(g_raw[:, k, :], g_raw[:, k, :], g_mean, ALU.subtract)
                last.then_inc(c_gc, 1)
                dve.wait_ge(c_c2, 1)
                v.tensor_copy(c2[:, :], B1[:, 0:F])
                dve.wait_ge(c_u, 1)
                for m in range(KF):
                    last = v.tensor_copy(w3_raw[:, m, 3 * F:3 * F + 2], A3[:, 2 * m:2 * m + 2])
                last.then_inc(c_u3, 1)
                dve.wait_ge(c_e, 1)
                v.tensor_copy(e_const[:, :], B3[:, 0:2])
                v.tensor_scalar(b2_half[:, :], b2_half[:, :], 0.5, None, ALU.mult)
                v.tensor_tensor(bk_sum[:, :], bk_raw[:, 0, :], bk_raw[:, 1, :], ALU.add).then_inc(c_dve, 1)
                dve.wait_ge(c_dve, 2)
                v.tensor_tensor(e_bias[:, :], e_const[:, 0:1], e_const[:, 1:2], ALU.add)
                v.tensor_tensor(bk_sum[:, :], bk_sum[:, :], bk_raw[:, 2, :], ALU.add).then_inc(c_dve, 1)
                dve.wait_ge(c_dve, 3)
                v.tensor_tensor(e_bias[:, :], e_bias[:, :], ab_b[:, :], ALU.add)
                dve.wait_ge(c_act, 2)
                low(gl[:, :, 0:F], g_raw[:, :, :], gh[:, :, 0:F])
                dve.wait_ge(c_act, 3)
                dve.wait_ge(c_l2, 1)
                low(w2l[:, :, :], l2_raw[:, :, :], w2h[:, :, :])
                dve.wait_ge(c_act, 4)
                dve.wait_ge(c_u3, 1)
                low(w3l[:, :, :], w3_raw[:, :, :], w3h[:, :, :]).then_inc(c_const, 1)

            def l0_h(b):
                s, h = b.slot(RING), b.slot(2)
                dve.wait_ge(at_in[s], b.dma_done(RING))
                for k in range(KN):
                    last = v.tensor_scalar(ht[:, h, k, :], at[:, s, k, :], 0.0, None, ALU.not_equal, ALU.add,
                                           accum_out=cnt[:, k:k + 1])
                last.then_inc(s_ht, 1)
                ready(dve, s_ht, b)
                v.tensor_scalar(be0[:, :], cnt[:, :], 1.0, None, ALU.max).then_inc(s_cntmax, 1)
                ready(dve, s_cntmax, b)
                v.reciprocal(be[:, :], be0[:, :]).then_inc(s_be, 1)

            def l0_zl(b):
                for m, ps in enumerate((A0, B0)):
                    dve.wait_ge(s_zh, b.number() * KN + m + 1)
                    last = low(zl[:, m, 0:F], ps[:, F:2 * F], zh[:, m, 0:F])
                last.then_inc(s_zl, 1)

            def l0_t(b):
                ready(dve, s_azmm, b)
                for m, ps in enumerate((A0, B0)):
                    last = v.tensor_scalar(deg[:, m:m + 1], ps[:, F:F + 1], EPS_DEG, None, ALU.max)
                last.then_inc(s_deg, 1)
                ready(dve, s_deg, b)
                v.reciprocal(rdeg[:, :], deg[:, :]).then_inc(s_rdeg, 1)
                ready(dve, s_rdeg, b)
                for m, ps in enumerate((A0, B0)):
                    last = v.scalar_tensor_tensor(t0[:, m, :], ps[:, 0:F], rdeg[:, m:m + 1], t0[:, m, :],
                                                  ALU.mult, ALU.add)
                last.then_inc(s_r0, 1)
                ready(dve, s_r0, b)
                s = b.slot(RING)
                dve.wait_ge(xm_in[s], b.dma_done(RING))
                v.scalar_tensor_tensor(t0[:, :, :], t0[:, :, :], 0.0,
                                       xm[:, s, 0:KN * F].rearrange("p (m f) -> p m f", f=F),
                                       ALU.max, ALU.add).then_inc(s_t0, 1)

            def l0_stats(b):
                row_stats(t0, bn0, mv0, s_t0, s_bn0, s_mv0, b)

            def l0_shift(b):
                shift(mv0, rs0, nm0, s_rs0, s_nm0, b)

            def l0_dn(b):
                ready(dve, s_dnmm, b)
                ready(dve, s_azmm, b)
                v.tensor_reduce(dn[:, :], DN, AX.X, ALU.add).then_inc(s_dn, 1)
                ready(dve, s_dn, b)
                v.tensor_scalar(dpos[:, :], dn[:, :], 0.0, None, ALU.is_gt)
                v.tensor_scalar(dmax[:, :], dn[:, :], TINY, None, ALU.max).then_inc(s_dpos, 1)
                ready(dve, s_dpos, b)
                v.reciprocal(drec[:, :], dmax[:, :]).then_inc(s_drec, 1)
                ready(dve, s_drec, b)
                v.tensor_tensor(dnr[:, :], drec[:, :], dpos[:, :], ALU.mult).then_inc(s_dnr, 1)
                ready(dve, s_dnr, b)
                v.tensor_copy(dnb[:, :, :], dnr[:, :].unsqueeze(2).to_broadcast([P, KN, P])).then_inc(s_dnb, 1)

            def l0_hb(b):
                ready(dve, s_dntr, b)
                ready(dve, s_be, b)
                h = b.slot(2)
                for k in range(KN):
                    last = v.scalar_tensor_tensor(hb[:, k, :], f(ht[:, h, k, :]), be[:, k:k + 1], B0[:, 0:N],
                                                  ALU.mult, ALU.mult)
                last.then_inc(s_hb, 1)

            def l1_sl(b):
                ready(dve, s_sh, b)
                low(sl[:, :, :], tiles(A1), sh[:, :, :]).then_inc(s_sl, 1)

            def l1_sxl(b):
                ready(dve, s_sxh, b)
                low(sxl[:, :, :], tiles(B1), sxh[:, :, :]).then_inc(s_sxl, 1)

            def l1_r1l(b):
                dve.wait_ge(s_r1h2, b.number() * 2 + 2)
                low(r1l[:, 2:4, :], r1[:, 2:4, :], r1h[:, 2:4, :]).then_inc(s_r1l, 1)

            def l1_hidden_var(b):
                ready(dve, s_vmm, b)
                for m, ps in enumerate((A1, B1)):
                    last = v.tensor_scalar(mu1[:, m:m + 1], ps[:, F:F + 1], 1.0 / H1, None, ALU.mult)
                last.then_inc(s_mu, 1)
                ready(dve, s_mu, b)
                v.tensor_tensor(mq1[:, :], mu1[:, :], mu1[:, :], ALU.mult).then_inc(s_mq, 1)
                ready(dve, s_mq, b)
                for m, ps in enumerate((A1, B1)):
                    last = v.scalar_tensor_tensor(var1[:, m:m + 1], ps[:, NO:NO + 1], 1.0 / H1, mq1[:, m:m + 1],
                                                  ALU.mult, ALU.subtract)
                last.then_inc(s_var, 1)
                ready(dve, s_var, b)
                v.tensor_scalar(vc1[:, :], var1[:, :], 0.0, None, ALU.max).then_inc(s_vc, 1)

            def l1_u(b):
                ready(dve, s_rsh, b)
                for m, ps in enumerate((A1, B1)):
                    last = v.scalar_tensor_tensor(u[:, m, :], ps[:, 0:F], rsh[:, m:m + 1], c2[:, :],
                                                  ALU.mult, ALU.add)
                last.then_inc(s_u, 1)

            def l1_t(b):
                ready(dve, s_ymm, b)
                ready(dve, s_x1b, b)
                v.scalar_tensor_tensor(t1[:, :, :], t1[:, :, :], 2.0, tiles(A1), ALU.mult, ALU.add).then_inc(s_t1, 1)

            def l1_stats(b):
                row_stats(t1, bn1, mv1, s_t1, s_bn1, s_mv1, b)

            def l1_x2(b):
                normalise(t1, mv1, rs1, x2[:, b.slot(2), :, :], s_rs1, s_x2, b)

            def l1_x2ml(b):
                ready(dve, s_x2mh, b)
                for m in range(KN):
                    last = v.scalar_tensor_tensor(x2ml[:, m, :], x2[:, b.slot(2), m, :], mask_of(b, m),
                                                  f(x2mh[:, m, :]), ALU.mult, ALU.subtract)
                last.then_inc(s_x2ml, 1)

            def l2_x2tl(b):
                ready(dve, s_x2th, b)
                low(x2tl[:, :, :], tiles(A2), x2th[:, :, :]).then_inc(s_x2tl, 1)

            def l2_w(b):
                ready(dve, s_aggmm, b)
                ready(dve, s_qv, b)
                for m in range(KN):
                    last = v.scalar_tensor_tensor(qv[:, m, 0:F], tiles(B2)[:, m, :], mask_of(b, m), qv[:, m, 0:F],
                                                  ALU.mult, ALU.mult, accum_out=wdot[:, m:m + 1])
                last.then_inc(s_w2, 1)
                ready(dve, s_w2, b)
                v.tensor_copy(wb[:, :, :], wdot[:, :].unsqueeze(2).to_broadcast([P, KN, P])).then_inc(s_wb, 1)

            def l2_max(b):
                ready(dve, s_wtr, b)
                v.tensor_reduce(mx[:, :], A2[:, 0:N], AX.X, ALU.max).then_inc(s_mx, 1)
                ready(dve, s_mx, b)
                v.tensor_scalar(nmx[:, :], mx[:, :], -1.0, None, ALU.mult).then_inc(s_nmx, 1)

            def l2_t(b):
                ready(dve, s_esum, b)
                v.reciprocal(ercp[:, :], esum[:, :]).then_inc(s_ercp, 1)
                ready(dve, s_ercp, b)
                v.tensor_scalar(aw[:, :], ew[:, :], ercp[:, 0:1], None, ALU.mult).then_inc(s_a, 1)
                ready(dve, s_a, b)
                for m in range(KN):
                    last = v.scalar_tensor_tensor(t2[:, m, :], t2[:, m, :], aw[:, m:m + 1],
                                                  x2[:, b.slot(2), m, :], ALU.mult, ALU.add)
                last.then_inc(s_t2, 1)

            def l2_stats(b):
                row_stats(t2, bn2, mv2, s_t2, s_bn2, s_mv2, b)

            def l2_shift(b):
                shift(mv2, rs2, nm2, s_rs2, s_nm2, b)

            def l3_x3tl(b):
                ready(dve, s_x3th, b)
                low(x3tl[:, :, :], tiles(A3), x3th[:, :, :]).then_inc(s_x3tl, 1)

            def l3_y2l(b):
                ready(dve, s_y2h, b)
                reuse(dve, s_ez, b)
                for m, ps in enumerate((B3, A3)):
                    v.tensor_scalar(sj[:, m:m + 1], ps[:, F:F + 1], e_bias[:, 0:1], None, ALU.add)
                    last = v.tensor_copy(sib[:, m, :], ps[:, F + 1:F + 2].to_broadcast([P, P]))
                last.then_inc(s_sib, 1)
                for m, ps in enumerate((B3, A3)):
                    last = low(y2l[:, m, 0:F], ps[:, 0:F], y2h[:, m, 0:F])
                last.then_inc(s_y2l, 1)

            def l3_leaky(b):
                ready(dve, s_ez, b)
                v.scalar_tensor_tensor(al[:, :, :], al[:, :, :], SLOPE, al[:, :, :], ALU.mult, ALU.max).then_inc(s_el, 1)

            def l3_z3(b):
                ready(dve, s_p2mm, b)
                for m, ps in enumerate((A3, B3)):
                    last = v.tensor_scalar(rsum[:, m:m + 1], ps[:, F:F + 1], EPS_SUM, None, ALU.add)
                last.then_inc(s_rsum, 1)
                ready(dve, s_rsum, b)
                v.reciprocal(rrec[:, :], rsum[:, :]).then_inc(s_rrec, 1)
                ready(dve, s_rrec, b)
                for m, ps in enumerate((A3, B3)):
                    last = v.scalar_tensor_tensor(z3[:, m, :], ps[:, 0:F], rrec[:, m:m + 1], z3[:, m, :],
                                                  ALU.mult, ALU.add)
                last.then_inc(s_z3, 1)

            def l3_t(b):
                ready(dve, s_p1mm, b)
                ready(dve, s_y0b, b)
                for m in range(KN):
                    last = v.scalar_tensor_tensor(t3[:, m, :], tiles(A3)[:, m, :], rrec[:, m:m + 1], t3[:, m, :],
                                                  ALU.mult, ALU.add)
                last.then_inc(s_r3, 1)
                ready(dve, s_r3, b)
                v.scalar_tensor_tensor(t3, t3, 0.0, x3[:, b.slot(2), :, :],
                                       ALU.max, ALU.add).then_inc(s_t3, 1)

            def l3_stats(b):
                row_stats(t3, bn3, mv3, s_t3, s_bn3, s_mv3, b)

            def l3_shift(b):
                shift(mv3, rs3, nm3, s_rs3, s_nm3, b)

            stages = [
                (l1_x2ml, 2), (l1_r1l, 1), (l0_stats, 0), (l0_hb, 0), (l0_h, -1), (l0_shift, 0),
                (l1_hidden_var, 1), (l2_w, 2), (l1_u, 1), (l2_max, 2), (l3_z3, 3), (l2_t, 2), (l2_stats, 2),
                (l1_t, 1), (l2_shift, 2), (l0_zl, -1), (l3_t, 3), (l1_sl, 0), (l1_stats, 1), (l3_x3tl, 2),
                (l1_x2, 1), (l1_sxl, 0), (l3_stats, 3), (l3_y2l, 2), (l2_x2tl, 1), (l3_shift, 3), (l0_dn, -1),
                (l0_t, -1), (l3_leaky, 2),
            ]

            constants()
            steps_of(dve, stages)

        @block.gpsimd
        def _(pool):
            g = nc.gpsimd

            def l0_split_at(b):
                s = b.slot(RING)
                ready(pool, s_ath, b)
                g.tensor_tensor(atl[:, s, :, :], at[:, s, :, :], f(ath[:, s, :, :]), ALU.subtract).then_inc(s_atl, 1)
                ready(pool, s_atl, b)
                reuse(pool, s_dnmm, b)
                first, first_l = at[:, s, :, 0:1], f(atl[:, s, :, 0:1])
                g.tensor_tensor(wcol[:, :, 0:1], first, first_l, ALU.subtract)
                g.tensor_tensor(wcol[:, :, 1:2], first, f(ath[:, s, :, 0:1]), ALU.subtract).then_inc(s_wcol, 1)

            def low(out, whole, high):
                return g.tensor_tensor(out, whole, f(high), ALU.subtract)

            def l0_hbl(b):
                ready(pool, s_hbh, b)
                low(hbl[:, :, :], hb[:, :, :], hbh[:, :, :]).then_inc(s_hbl, 1)

            def l0_split_x(b):
                ready(pool, s_x0th, b)
                low(x0tl[:, :, :], xt[:, b.slot(2), :, :], x0th[:, :, :]).then_inc(s_x0tl, 1)

            def l0_x1l(b):
                ready(pool, s_x1h, b)
                low(x1l[:, :, :], x1[:, :, :], x1h[:, :, :]).then_inc(s_x1l, 1)

            def l1_r1l(b):
                pool.wait_ge(s_r1h2, b.number() * 2 + 1)
                low(r1l[:, 0:2, :], r1[:, 0:2, :], r1h[:, 0:2, :]).then_inc(s_r1l2, 1)

            def l1_ul(b):
                ready(pool, s_uh, b)
                low(ul[:, :, :], u[:, :, :], uh[:, :, :]).then_inc(s_ul, 1)

            def l3_alpha(b):
                ready(pool, s_ee, b)
                g.tensor_tensor(al[:, :, :], al[:, :, :], at[:, b.slot(RING), :, :], ALU.mult).then_inc(s_al, 1)

            def l3_all(b):
                ready(pool, s_alh, b)
                low(all_[:, :, :], al[:, :, :], alh[:, :, :]).then_inc(s_all, 1)

            def l3_z3l(b):
                ready(pool, s_z3h, b)
                low(z3l[:, :, :], z3, z3h[:, :, :]).then_inc(s_z3l, 1)

            def l1_x1b(b):
                ready(pool, s_x1, b)
                reuse(pool, s_x2, b)
                g.tensor_tensor(t1[:, :, :], x1[:, :, :], b2_half[:, :].unsqueeze(1).to_broadcast([P, KN, F]), ALU.add).then_inc(s_x1b, 1)

            def l1_sumsq(b):
                ready(pool, s_sq, b)
                g.tensor_tensor(sq[:, 0:2, :], sq[:, 0:2, :], sq[:, 2:4, :], ALU.add).then_inc(s_sq2, 1)
                ready(pool, s_sq2, b)
                reuse(pool, s_vmm, b)
                g.tensor_tensor(sq1[:, :], sq[:, 0, :], sq[:, 1, :], ALU.add).then_inc(s_sq1, 1)

            def l3_y0b(b):
                ready(pool, s_y01, b)
                g.tensor_tensor(t3, t3, bk_sum[:, :].unsqueeze(1).to_broadcast([P, KN, F]), ALU.add).then_inc(s_y0b, 1)

            stages = [
                (l1_r1l, 1), (l3_alpha, 3), (l1_sumsq, 1), (l3_all, 3), (l0_split_x, -1), (l3_y0b, 3),
                (l0_hbl, 0), (l1_ul, 1), (l3_z3l, 3), (l0_split_at, -1), (l0_x1l, 0), (l1_x1b, 0),
            ]

            pool.wait_ge(c_const, 1)
            steps_of(pool, stages)


def kernel(x, adj, nodemask, L0_gnn_W, L1_gnn_W1, L1_gnn_b1, L1_gnn_gamma, L1_gnn_beta, L1_gnn_W2, L1_gnn_b2,
           L2_gnn_Wqk, L2_gnn_Wv, L3_gnn_Wv, L3_gnn_bv, L3_gnn_aw, L3_gnn_ab, L3_gnn_Wk, L3_gnn_bk):
    import numpy as np
    import concourse.bacc as bacc
    from concourse.bass_utils import run_bass_kernel_spmd

    def rows(a):
        a = np.asarray(a)
        k = a.shape[-2] // P
        a = a.reshape(a.shape[:-2] + (k, P, a.shape[-1]))
        return np.ascontiguousarray(np.moveaxis(a, -3, -2))

    def column(a):
        return np.ascontiguousarray(np.asarray(a).reshape(-1, P).T)

    x, adj, nodemask = np.asarray(x), np.asarray(adj), np.asarray(nodemask)
    W, Wk = np.asarray(L0_gnn_W).T, np.asarray(L3_gnn_Wk)
    aw = np.asarray(L3_gnn_aw)[:, 0].reshape(2, KF, P)
    arrays = {
        "at": rows(np.swapaxes(adj, 1, 2)),
        "xt": rows(np.swapaxes(x, 1, 2)),
        "xm": np.concatenate([rows(x).reshape(B, P, KN * F),
                              np.swapaxes(nodemask.reshape(B, KN, P), 1, 2)], axis=2),
        "w_l0": rows(np.concatenate([W[0:F], W[F:2 * F]], axis=1)),
        "w1": rows(np.asarray(L1_gnn_W1).T),
        "w2": rows(np.asarray(L1_gnn_W2).T),
        "wqk": rows(np.asarray(L2_gnn_Wqk).T),
        "wv2": rows(L2_gnn_Wv),
        "w3": rows(np.concatenate([Wk[0], Wk[1], Wk[2]], axis=1)),
        "wv3": rows(np.asarray(L3_gnn_Wv).T),
        "aw": np.ascontiguousarray(np.transpose(aw, (2, 1, 0))),
        "cols": np.concatenate([column(L1_gnn_b1), column(L1_gnn_gamma), column(L1_gnn_beta), column(L3_gnn_bv)], axis=1),
        "b2": np.ascontiguousarray(np.broadcast_to(np.asarray(L1_gnn_b2), (P, F))),
        "bk": np.ascontiguousarray(np.broadcast_to(np.asarray(L3_gnn_bk), (P, 3, F))),
        "ab": np.ascontiguousarray(np.broadcast_to(np.asarray(L3_gnn_ab), (P, 1))),
        "ident": np.eye(P, dtype=np.float32),
    }
    nc = bacc.Bacc("TRN2", target_bir_lowering=False, num_devices=1)
    arrays = {f"in_{k}": np.ascontiguousarray(a) for k, a in arrays.items()}
    args = [nc.dram_tensor(k, a.shape, mybir.dt.from_np(a.dtype), kind="ExternalInput").ap() for k, a in arrays.items()]
    args.append(nc.dram_tensor("out", (B, P, KN, F), F32, kind="ExternalOutput").ap())
    resnorm_kernel(nc, *args)
    r = run_bass_kernel_spmd(nc, [arrays], core_ids=[0])
    out = r.results[0]["out"]
    return np.ascontiguousarray(np.moveaxis(out, 2, 1).reshape(B, N, F))
```

```python
import math

import concourse.bass as bass
from concourse import mybir
from contextlib import ExitStack

F32 = mybir.dt.float32
F32R = mybir.dt.float32r
ALU = mybir.AluOpType
ACT = mybir.ActivationFunctionType
AX = mybir.AxisListType

P = 128
B, N, F = 32, 256, 256
KN = N // P
KF = F // P
H1 = 512
KH = H1 // P
NO = N + 2
RING = 4
MIN_SKEW, MAX_SKEW = -2, 3
EPS_DEG, EPS_LN, EPS_SUM = 1e-6, 1e-5, 1e-12
TINY = 1.2e-38
SLOPE = 0.2

NEWTON_A = 0.5 ** (1 / 3)
NEWTON_S = 1.5 / NEWTON_A



class Batch:

    def __init__(self, i, c):
        self.i, self.c = i, c
        self.is_first = isinstance(i, int) and c == 0

    def follows(self, n):
        return not isinstance(self.i, int) or self.c >= n

    def number(self):
        return self.i * RING + self.c

    def count(self, n, k):
        return self.i * (RING * n) + (self.c * n + k)

    def done(self):
        return self.count(1, 1)

    def before(self, d=0):
        return self.count(1, -d)

    def slot(self, ring):
        return self.c % ring

    def dma_done(self, ring):
        return self.i * (16 * RING // ring) + 16 * (self.c // ring + 1)


class Step:

    def __init__(self, sem, k, n):
        self.sem, self.k, self.n = sem, k, n

    def done(self, b):
        return b.count(self.n, self.k + 1)


class Norm:

    def __init__(self, name, sb, sem, chain, t, s_t, var=None):
        def col(what):
            return sb(f"{name}_{what}", [P, KN])

        self.t, self.s_t, self.var = t, s_t, var
        if var is None:
            self.bn, self.mv, self.shift = sb(f"{name}_bn", [P, KN, 6]), sb(f"{name}_mv", [P, KN, 2]), col("shift")
            self.mean, self.var = self.mv[:, :, 0], self.mv[:, :, 1]
            self.s_bn = sem(f"{name}_stats_ready")
        self.lnv, self.guess, self.va, self.rs = col("lnv"), col("guess"), col("va"), col("rstd")
        steps = chain(f"{name}_step", 6 if var is not None else 7)
        self.s_mv, self.s_lnv, self.s_guess, self.s_va, self.s_vaa, self.s_rs = steps[:6]
        self.s_shift = steps[-1]


def steps_of(eng, stages, after_first=()):
    def run(batch):
        for stage, *norm, skew in stages:
            b = batch(skew)
            if b:
                stage(*norm, b)
                if b.is_first and stage in after_first:
                    after_first[stage]()

    head = MAX_SKEW + 2
    rounds = (B + MIN_SKEW - head) // RING
    for t in range(MIN_SKEW, head):
        run(lambda skew, t=t: Batch(0, t - skew) if t >= skew else None)
    with eng.Fori(0, rounds) as i:
        for u in range(RING):
            run(lambda skew, u=u: Batch(i, head + u - skew))
    for t in range(head + rounds * RING, B + MAX_SKEW):
        run(lambda skew, t=t: Batch(0, t - skew) if t - skew < B else None)


def resnorm_kernel(nc, at_d, xt_d, xm_d, w_l0_d, w1_d, w2_d, wqk_d, wv2_d, w3_d, wv3_d,
                   aw_d, cols_d, b2_d, bk_d, ab_d, ident_d, out_d):
    ctx = ExitStack()
    with ctx:
        def sb(name, shape, dt=F32):
            return ctx.enter_context(nc.sbuf_tensor(name, shape, dt))

        def sem(name):
            return ctx.enter_context(nc.semaphore(name))

        def sems(names):
            return [sem(n) for n in names.split()]

        ident = sb("ident", [P, P])
        ones = sb("ones", [P, P])
        eps_ln, ln_a = sb("eps_ln", [P, 1]), sb("ln_a", [P, 1])
        w3_raw = sb("w3_raw", [P, KF, 3 * F + 2])
        aw_raw = sb("aw_raw", [P, KF, 2])
        cols = sb("cols", [P, 14])
        b1c, gammac, betac, bvc = cols[:, 0:4], cols[:, 4:8], cols[:, 8:12], cols[:, 12:14]
        b2_half = sb("b2_half", [P, F])
        bk_sum = sb("bk_sum", [P, F])
        ab_b = sb("ab_b", [P, 1])
        c2 = sb("c2", [P, F])
        e_const = sb("e_const", [P, 2])
        e_bias = sb("e_bias", [P, 1])
        w0h, w0l = sb("w0h", [P, KF, 2 * F], F32R), sb("w0l", [P, KF, 2 * F], F32R)
        w1h, w1l = sb("w1h", [P, KF, H1], F32R), sb("w1l", [P, KF, H1], F32R)
        gh, gl = sb("gh", [P, KH, NO], F32R), sb("gl", [P, KH, NO], F32R)
        w2h, w2l = sb("w2h", [P, KF, 2 * F], F32R), sb("w2l", [P, KF, 2 * F], F32R)
        w3h, w3l = sb("w3h", [P, KF, 3 * F + 2], F32R), sb("w3l", [P, KF, 3 * F + 2], F32R)

        at = sb("at", [P, RING, KN, N])
        ath, atl = sb("ath", [P, RING, KN, N], F32R), sb("atl", [P, RING, KN, N], F32R)
        xt = sb("xt", [P, 2, KF, N])
        xm = sb("xm", [P, RING, KN * F + KN])

        x0th, x0tl = sb("x0th", [P, KF, N], F32R), sb("x0tl", [P, KF, N], F32R)
        t0 = sb("t0", [P, KN, F])
        zh, zl = sb("zh", [P, KN, NO], F32R), sb("zl", [P, KN, NO], F32R)
        deg, rdeg = sb("deg", [P, KN]), sb("rdeg", [P, KN])
        ht = sb("ht", [P, 2, KN, N], F32R)
        cnt, be0, be = sb("cnt", [P, KN]), sb("be0", [P, KN]), sb("be", [P, KN])
        wcol = sb("wcol", [P, KN, 2], F32R)
        dn, dmax, drec = sb("dn", [P, KN]), sb("dmax", [P, KN]), sb("drec", [P, KN])
        dnb = sb("dnb", [P, KN, P])
        hb = sb("hb", [P, KN, N])
        hbh, hbl = sb("hbh", [P, KN, N], F32R), sb("hbl", [P, KN, N], F32R)
        x1 = sb("x1", [P, KN, F])
        x1h, x1l = sb("x1h", [P, KN, F], F32R), sb("x1l", [P, KN, F], F32R)

        sh, sl = sb("sh", [P, 2, KN, N], F32R), sb("sl", [P, 2, KN, N], F32R)
        sxh, sxl = sb("sxh", [P, KF, N], F32R), sb("sxl", [P, KF, N], F32R)
        r1 = sb("r1", [P, KH, N])
        r1h, r1l = sb("r1h", [P, KH, N], F32R), sb("r1l", [P, KH, N], F32R)
        sq = sb("sq", [P, KH, N])
        sq1 = sb("sq1", [P, N])
        mu1, mq1, var1, vc1 = sb("mu1", [P, KN]), sb("mq1", [P, KN]), sb("var1", [P, KN]), sb("vc1", [P, KN])
        u = sb("u", [P, KN, F])
        uh, ul = sb("uh", [P, KN, F], F32R), sb("ul", [P, KN, F], F32R)
        t1 = sb("t1", [P, KN, F])
        x2 = sb("x2", [P, 2, KN, F])
        x2mh, x2ml = sb("x2mh", [P, KN, F], F32R), sb("x2ml", [P, KN, F], F32R)

        x2th, x2tl = sb("x2th", [P, KF, N], F32R), sb("x2tl", [P, KF, N], F32R)
        qv = sb("qv", [P, KN, 2 * F])
        wdot = sb("wdot", [P, KN])
        wb = sb("wb", [P, KN, P])
        nmx = sb("nmx", [P, 1])
        ejunk, esum, ercp = sb("ejunk", [P, N]), sb("esum", [P, 1]), sb("ercp", [P, 1])
        ew, aw = sb("ew", [P, KN]), sb("aw", [P, KN])
        t2 = qv[:, :, F:2 * F]
        x3 = sb("x3", [P, 2, KN, F])

        x3th, x3tl = sb("x3th", [P, KF, N], F32R), sb("x3tl", [P, KF, N], F32R)
        y2h, y2l = sb("y2h", [P, KN, NO], F32R), sb("y2l", [P, KN, NO], F32R)
        sj = sb("sj", [P, KN])
        sib = sb("sib", [P, KN, P])
        y01 = sb("y01", [P, KN, 2 * F])
        t3 = y01[:, :, 0:F]
        z3 = y01[:, :, F:2 * F]
        al = sb("al", [P, KN, N])
        alh, all_ = sb("alh", [P, KN, N], F32R), sb("all", [P, KN, N], F32R)
        rsum, rrec = sb("rsum", [P, KN]), sb("rrec", [P, KN])
        z3h, z3l = sb("z3h", [P, KN, F], F32R), sb("z3l", [P, KN, F], F32R)
        xo = sb("xo", [P, 2, KN, F])

        def over(tile, k):
            return tile.rearrange("p a b -> p (a b)").rearrange("p (k f) -> p k f", k=k)

        def slots(tile):
            return tile[:, 0:2, :, :].rearrange("p a b c -> p a (b c)")

        w0_raw, w1_raw = over(slots(x3), KF), over(slots(xo), KF)
        w2_raw, g_raw, wqk_raw, l2_raw = r1[:, :, :], sq[:, :, :], over(qv[:, :, :], KH), y01[:, :, :]
        wv3_raw, beta_b, bv_b = t1[:, :, :], over(u[:, :, :], KH), al[:, :, 0:P]
        bk_raw = over(slots(x2), KH)[:, 0:3, :]
        g_mean = ejunk[:, :]

        bank = [ctx.enter_context(nc.psum_tensor(f"bank{i}", [P, 512], F32)) for i in range(8)]
        A0, B0, A1, B1, A2, B2, A3, B3 = bank
        DN = A0[:, 264:264 + 2 * KN].rearrange("p (m c) -> p m c", c=2)

        def tiles(ps, n=KN, w=F):
            return ps[:, 0:n * w].rearrange("p (m f) -> p m f", f=w)

        def f(ap):
            return ap.bitcast(F32)

        def chain(name, n):
            s = sem(name)
            return [Step(s, k, n) for k in range(n)]

        w_in = [sem(f"weights{n}_loaded") for n in range(4)]
        s_memset = sem("constants_set")
        c_w0h, c_w0 = sem("w0h_ready"), sem("w0_ready")
        c_w1h, c_w1 = sem("w1h_ready"), sem("w1_ready")
        c_gamma, c_beta, c_mean, c_gmean, c_gc, c_gh, c_g = sems(
            "gamma_w2_ready beta_ready gamma_w2_sums_done gamma_w2_means_ready g_ready gh_ready g_split")
        c_c2mm, c_c2 = sem("beta_w2_done"), sem("c2_ready")
        c_m, c_m2, c_w2h, c_w2 = sems("qk_done qk_ready w2h_ready w2_ready")
        c_bv, c_u, c_e, c_u3, c_w3h, c_w3 = sems("bv_ready wva_done bva_done wva_ready w3h_ready w3_ready")
        c_sum, c_bias = sem("bias_sums_ready"), sem("biases_ready")
        at_in = [sem(f"at_in{i}") for i in range(RING)]
        xt_in = [sem(f"xt_in{i}") for i in range(2)]
        ident_in = sem("ident_loaded")
        xm_in = [sem(f"xm_in{i}") for i in range(RING)]
        stored = [sem(f"stored{i}") for i in range(2)]
        s_x0th, s_x0tl, s_ath, s_atl, s_ht = sems(
            "x0th_ready x0tl_ready ath_ready atl_ready ht_ready")
        s_wcol = sem("wcol_ready")
        s_y0mm, s_zh, s_zl, s_azmm, s_r0 = sems(
            "y0_done zh_ready zl_ready az_done r0_ready")
        s_t0 = sem("t0_ready")
        s_x1, s_x1h, s_x1l = sems(
            "x1_ready x1h_ready x1l_ready")
        s_dnmm, s_dnb, s_dntr, s_hb, s_hbh = sems(
            "dn_done dnb_ready dnb_transposed hb_ready hbh_ready")
        s_hbl = sem("hbl_ready")
        s_smm, s_sh, s_sl, s_sxmm, s_sxh = sems(
            "s_done sh_ready sl_ready sx_done sxh_ready")
        s_sxl, s_rmm, s_r1, s_r1l = sems(
            "sxl_ready r_done r1_halves_ready r1l_second_half_ready")
        s_sq, s_sq2, s_sq1, s_vmm = sems(
            "sq_ready sq2_ready sq1_ready v_done")
        s_u, s_uh, s_ul, s_x1b, s_ymm = sems(
            "u_ready uh_ready ul_ready x1b_ready y_done")
        s_t1, s_x2, s_x2mh, s_x2ml = sems(
            "t1_ready x2_ready x2mh_ready x2ml_ready")
        s_x2tr, s_x2th, s_x2tl, s_qvmm, s_qv = sems(
            "x2_transposed x2th_ready x2tl_ready qv_done qv_ready")
        s_aggmm, s_w2, s_wb, s_wtr, s_esum = sems(
            "agg_done w_ready wb_ready w_transposed exps_ready")
        s_t2, s_x3 = sems(
            "t2_ready x3_ready")
        s_x3tr, s_x3th, s_x3tl, s_y2mm, s_y2h = sems(
            "x3_transposed x3th_ready x3tl_ready y2_done y2h_ready")
        s_y2l, s_sib, s_sitr, s_ez, s_el = sems(
            "y2l_ready sib_ready si_transposed ez_ready el_ready")
        s_ee, s_al, s_alh, s_all = sems(
            "ee_ready alpha_ready alh_ready all_ready")
        s_y01mm, s_y01, s_y0b, s_p2mm, s_z3 = sems(
            "y01_done y01_ready y0b_ready p2_done z3_ready")
        s_z3h, s_z3l, s_p1mm, s_r3, s_t3 = sems(
            "z3h_ready z3l_ready p1_done r3_ready t3_ready")
        s_xo = sem("out_ready")

        s_r1h2, s_r1l2 = sems(
            "r1h_half_ready r1l_first_half_ready")

        s_mu, s_mq, s_var = chain("hidden_var_step", 3)
        HIDDEN = 4
        norms = [Norm(f"norm{n}", sb, sem, chain, t, s_t)
                 for n, (t, s_t) in enumerate(((t0, s_t0), (t1, s_t1), (t2, s_t2), (t3, s_t3)))]
        norms.append(Norm("hidden", sb, sem, chain, None, None, vc1[:, :]))
        s_dn, s_dmax, s_drec = chain("dn_step", 3)
        s_cntmax, s_be = chain("edge_weight_step", 2)
        s_deg, s_rdeg = chain("degree_step", 2)
        s_nmx = sem("logit_max_ready")
        s_ercp, s_a = chain("softmax_scale_step", 2)
        s_rsum, s_rrec = chain("row_sum_step", 2)

        def mask_of(b, m):
            return xm[:, b.slot(RING), KN * F + m:KN * F + m + 1]

        def ready(eng, s, b):
            if isinstance(s, Step):
                eng.wait_ge(s.sem, s.done(b))
            else:
                eng.wait_ge(s, b.done())

        def reuse(eng, s, b):
            if b.follows(1):
                eng.wait_ge(s, b.before())

        block = ctx.enter_context(nc.Block())

        n_parameters = (1, 4, 2, 5)

        @block.sync
        def _(sp):
            def load_at(b):
                sp.dma_start(at[:, b.slot(RING), :, :], at_d[b.number(), :, :, :]).then_inc(at_in[b.slot(RING)], 16)

            def load_xt(b):
                sp.dma_start(xt[:, b.slot(2), :, :], xt_d[b.number(), :, :, :]).then_inc(xt_in[b.slot(2)], 16)

            def load_xm(b):
                sp.dma_start(xm[:, b.slot(RING), :], xm_d[b.number(), :, :]).then_inc(xm_in[b.slot(RING)], 16)

            parameters = (
                ((w0_raw, w_l0_d),),
                ((cols[:, :], cols_d), (w2_raw, w2_d), (w1_raw, w1_d), (b2_half[:, :], b2_d)),
                ((wqk_raw, wqk_d), (l2_raw[:, :, F:2 * F], wv2_d)),
                ((aw_raw[:, :, :], aw_d), (wv3_raw, wv3_d), (w3_raw[:, :, 0:3 * F], w3_d), (bk_raw, bk_d),
                 (ab_b[:, :], ab_d)))

            def load_parameters(n):
                for dst, src in parameters[n]:
                    sp.dma_start(dst, src).then_inc(w_in[n], 16)

            def load_others():
                sp.dma_start(ident[:, :], ident_d).then_inc(ident_in, 16)
                for n in (1, 2, 3):
                    load_parameters(n)

            def load_x(b):
                if b.follows(2):
                    sp.wait_ge(s_x0tl, b.before(1))
                load_xt(b)
                if b.follows(RING):
                    sp.wait_ge(s_w2, b.before(RING - 1))
                    sp.wait_ge(s_x2ml, b.before(RING - 1))
                load_xm(b)

            def load_adj(b):
                if b.follows(RING):
                    sp.wait_ge(s_al, b.before(RING - 1))
                load_at(b)

            def store(b):
                ready(sp, s_xo, b)
                sp.dma_start(out_d[b.number(), :, :, :], xo[:, b.slot(2), :, :]).then_inc(stored[b.slot(2)], 16)

            load_parameters(0)
            steps_of(sp, [(load_x, -2), (load_adj, -2), (store, 3)], {load_adj: load_others})
            for s in stored:
                sp.wait_ge(s, 16 * B // 2)

        @block.tensor
        def _(pe):
            def mm(out, lhs, rhs, start, stop):
                return nc.tensor.matmul(out, lhs, rhs, start=start, stop=stop)

            def product(out, lhs, rhs, k_tiles):
                for k in range(k_tiles):
                    (lh, ll), (rh, rl) = lhs(k), rhs(k)
                    mm(out, lh, rh, k == 0, False)
                    mm(out, lh, rl, False, False)
                    last = mm(out, ll, rh, False, k == k_tiles - 1)
                return last

            def cut(m):
                return slice(m * P, (m + 1) * P)

            def transposes(ps, src):
                for m in range(KN):
                    for k in range(KF):
                        last = nc.tensor.transpose(tiles(ps)[:, k, cut(m)], src[:, m, cut(k)], ident[:, :])
                return last

            def constants_1():
                pe.wait_ge(c_gamma, 1)
                pe.wait_ge(s_memset, 1)
                for k in range(KH):
                    last = mm(A1[:, 0:F], ones[:, :], g_raw[:, k, :], k == 0, k == KH - 1)
                last.then_inc(c_mean, 1)
                pe.wait_ge(c_beta, 1)
                for k in range(KH):
                    last = mm(B1[:, 0:F], beta_b[:, k, :], w2_raw[:, k, :], k == 0, k == KH - 1)
                last.then_inc(c_c2mm, 1)

            def constants_2():
                pe.wait_ge(w_in[2], 16 * n_parameters[2])
                for m in range(KF):
                    for k in range(KF):
                        last = mm(tiles(A2)[:, m, :], wqk_raw[:, k, cut(m)], wqk_raw[:, KF + k, :], k == 0, k == KF - 1)
                last.then_inc(c_m, 1)

            def constants_3():
                pe.wait_ge(w_in[3], 16 * n_parameters[3])
                for m in range(KF):
                    for k in range(KF):
                        last = mm(A3[:, 2 * m:2 * m + 2], wv3_raw[:, k, cut(m)], aw_raw[:, k, :], k == 0, k == KF - 1)
                last.then_inc(c_u, 1)
                pe.wait_ge(c_bv, 1)
                for k in range(KF):
                    last = mm(B3[:, 0:2], bv_b[:, k, :], aw_raw[:, k, :], k == 0, k == KF - 1)
                last.then_inc(c_e, 1)

            def first(b, s, n=1):
                if b.is_first:
                    pe.wait_ge(s, n)

            def l0_y(b):
                reuse(pe, s_sl, b)
                reuse(pe, s_r0, b)
                ready(pe, s_x0tl, b)
                ready(pe, s_x0th, b)
                first(b, c_w0)
                for m, ps in enumerate((A0, B0)):
                    last = product(ps[:, :], lambda k: (x0th[:, k, cut(m)], x0tl[:, k, cut(m)]),
                                   lambda k: (w0h[:, k, :], w0l[:, k, :]), KF)
                    last.then_inc(s_y0mm, 1)

            def l0_az(b):
                first(b, s_memset)
                s = b.slot(RING)
                ready(pe, s_zl, b)
                ready(pe, s_atl, b)
                ready(pe, s_ath, b)
                for m, ps in enumerate((A0, B0)):
                    last = product(ps[:, 0:NO], lambda k: (ath[:, s, k, cut(m)], atl[:, s, k, cut(m)]),
                                   lambda k: (zh[:, k, :], zl[:, k, :]), KN)
                last.then_inc(s_azmm, 1)

            def l0_dn(b):
                h = b.slot(2)
                ready(pe, s_zl, b)
                ready(pe, s_ht, b)
                ready(pe, s_wcol, b)
                for m in range(KN):
                    for k in range(KN):
                        last = mm(DN[:, m, :], ht[:, h, k, cut(m)], wcol[:, k, :], k == 0, k == KN - 1)
                last.then_inc(s_dnmm, 1)

            def l0_dn_rows(b):
                first(b, ident_in, 16)
                ready(pe, s_dnb, b)
                ready(pe, s_r0, b)
                for m in range(KN):
                    last = nc.tensor.transpose(B0[:, cut(m)], dnb[:, m, :], ident[:, :])
                last.then_inc(s_dntr, 1)

            def l1_s(b):
                h = b.slot(2)
                ready(pe, s_hbl, b)
                ready(pe, s_hbh, b)
                ready(pe, s_ht, b)
                for m in range(KN):
                    for k in range(KN):
                        mm(tiles(B0)[:, m, :], ht[:, h, k, cut(m)], hbh[:, k, :], k == 0, False)
                        last = mm(tiles(B0)[:, m, :], ht[:, h, k, cut(m)], hbl[:, k, :], False, k == KN - 1)
                last.then_inc(s_smm, 1)

            def l1_sx(b):
                h = b.slot(2)
                ready(pe, s_sl, b)
                ready(pe, s_sh, b)
                ready(pe, s_x1l, b)
                ready(pe, s_x1h, b)
                reuse(pe, s_u, b)
                first(b, c_c2)
                for m in range(KF):
                    last = product(tiles(B1)[:, m, :], lambda k: (x1h[:, k, cut(m)], x1l[:, k, cut(m)]),
                                   lambda k: (sh[:, h, k, :], sl[:, h, k, :]), KN)
                last.then_inc(s_sxmm, 1)

            def l1_r(b):
                first(b, c_w1)
                first(b, c_gmean)
                first(b, c_c2)
                ready(pe, s_sxl, b)
                ready(pe, s_sxh, b)
                reuse(pe, s_t1, b)
                for m in range(KH):
                    last = product(tiles((A1, B1)[m // 2])[:, m % 2, :],
                                   lambda k: (w1h[:, k, cut(m)], w1l[:, k, cut(m)]),
                                   lambda k: (sxh[:, k, :], sxl[:, k, :]), KF)
                    if m % 2:
                        last.then_inc(s_rmm, 1)

            def l1_v(b):
                first(b, c_g)
                ready(pe, s_r1l2, b)
                ready(pe, s_r1l, b)
                for m, ps in enumerate((A1, B1)):
                    product(ps[:, 0:NO], lambda k: (r1h[:, k, cut(m)], r1l[:, k, cut(m)]),
                            lambda k: (gh[:, k, :], gl[:, k, :]), KH)
                ready(pe, s_sq1, b)
                for m, ps in enumerate((A1, B1)):
                    last = mm(ps[:, NO:NO + 1], sq1[:, cut(m)], ones[:, 0:1], True, True)
                last.then_inc(s_vmm, 1)

            def l1_y(b):
                h = b.slot(2)
                ready(pe, s_ul, b)
                ready(pe, s_uh, b)
                for m in range(KN):
                    last = product(tiles(A1)[:, m, :], lambda k: (sh[:, h, k, cut(m)], sl[:, h, k, cut(m)]),
                                   lambda k: (uh[:, k, :], ul[:, k, :]), KN)
                last.then_inc(s_ymm, 1)

            def l2_tr(b):
                first(b, c_m2)
                ready(pe, s_x2, b)
                reuse(pe, s_esum, b)
                transposes(A2, x2[:, b.slot(2), :, :]).then_inc(s_x2tr, 1)

            def l2_qv(b):
                first(b, c_w2)
                ready(pe, s_x2tl, b)
                ready(pe, s_x2th, b)
                reuse(pe, s_x3tl, b)
                for m, ps in enumerate((B2, A2)):
                    last = product(ps[:, :], lambda k: (x2th[:, k, cut(m)], x2tl[:, k, cut(m)]),
                                   lambda k: (w2h[:, k, :], w2l[:, k, :]), KF)
                    last.then_inc(s_qvmm, 1)

            def l2_agg(b):
                s = b.slot(RING)
                ready(pe, s_x2ml, b)
                ready(pe, s_x2mh, b)
                ready(pe, s_qv, b)
                for m in range(KN):
                    last = product(tiles(B2)[:, m, :], lambda k: (ath[:, s, k, cut(m)], atl[:, s, k, cut(m)]),
                                   lambda k: (x2mh[:, k, :], x2ml[:, k, :]), KN)
                last.then_inc(s_aggmm, 1)

            def l2_w_rows(b):
                ready(pe, s_wb, b)
                for m in range(KN):
                    last = nc.tensor.transpose(A2[:, cut(m)], wb[:, m, :], ident[:, :])
                last.then_inc(s_wtr, 1)

            def l3_tr(b):
                ready(pe, s_x3, b)
                transposes(B2, x3[:, b.slot(2), :, :]).then_inc(s_x3tr, 1)

            def l3_y2(b):
                first(b, c_w3)
                ready(pe, s_x3tl, b)
                ready(pe, s_x3th, b)
                reuse(pe, s_r3, b)
                for m, ps in enumerate((B3, A3)):
                    last = product(ps[:, 0:NO], lambda k: (x3th[:, k, cut(m)], x3tl[:, k, cut(m)]),
                                   lambda k: (w3h[:, k, 2 * F:3 * F + 2], w3l[:, k, 2 * F:3 * F + 2]), KF)
                    last.then_inc(s_y2mm, 1)

            def l3_si_rows(b):
                ready(pe, s_sib, b)
                ready(pe, s_y2l, b)
                for m in range(KN):
                    last = nc.tensor.transpose(B3[:, cut(m)], sib[:, m, :], ident[:, :])
                last.then_inc(s_sitr, 1)

            def l3_y01(b):
                ready(pe, s_y2l, b)
                ready(pe, s_ez, b)
                for m, ps in enumerate((A3, B3)):
                    last = product(ps[:, :], lambda k: (x3th[:, k, cut(m)], x3tl[:, k, cut(m)]),
                                   lambda k: (w3h[:, k, 0:2 * F], w3l[:, k, 0:2 * F]), KF)
                    last.then_inc(s_y01mm, 1)

            def l3_p2(b):
                ready(pe, s_all, b)
                ready(pe, s_alh, b)
                ready(pe, s_y2h, b)
                ready(pe, s_y01, b)
                for m, ps in enumerate((A3, B3)):
                    last = product(ps[:, 0:NO], lambda k: (alh[:, k, cut(m)], all_[:, k, cut(m)]),
                                   lambda k: (y2h[:, k, :], y2l[:, k, :]), KN)
                last.then_inc(s_p2mm, 1)

            def l3_p1(b):
                ready(pe, s_z3l, b)
                ready(pe, s_z3h, b)
                for m in range(KN):
                    last = product(tiles(A3)[:, m, :], lambda k: (alh[:, k, cut(m)], all_[:, k, cut(m)]),
                                   lambda k: (z3h[:, k, :], z3l[:, k, :]), KN)
                last.then_inc(s_p1mm, 1)

            stages = [
                (l2_agg, 2), (l3_y01, 3), (l1_s, 0), (l2_w_rows, 2), (l3_p2, 3), (l1_y, 1), (l0_y, -1),
                (l1_sx, 0), (l3_p1, 3), (l0_az, -1), (l0_dn, -1), (l3_tr, 2), (l2_tr, 1), (l1_r, 0), (l3_y2, 2),
                (l2_qv, 1), (l0_dn_rows, -1), (l3_si_rows, 2), (l1_v, 0),
            ]

            steps_of(pe, stages, {l0_y: constants_1, l0_dn: constants_2, l0_dn_rows: constants_3})

        @block.scalar
        def _(act):
            def copy(out, src, **kw):
                return nc.scalar.activation(out, src, ACT.Identity, **kw)

            def log_var(n, b):
                if b.is_first:
                    act.wait_ge(s_memset, 1)
                ready(act, norms[n].s_mv, b)
                nc.scalar.activation(norms[n].lnv[:, :], norms[n].var, ACT.Ln,
                                     bias=eps_ln[:, 0:1]).then_inc(norms[n].s_lnv.sem, 1)

            def guess(n, b):
                ready(act, norms[n].s_lnv, b)
                nc.scalar.activation(norms[n].guess[:, :], norms[n].lnv[:, :], ACT.Exp, scale=-0.5,
                                     bias=ln_a[:, 0:1]).then_inc(norms[n].s_guess.sem, 1)

            def normalise(n, out, s_out, b):
                ready(act, norms[n].s_shift, b)
                for m in range(KN):
                    last = copy(out[:, m, :], norms[n].t[:, m, :], bias=norms[n].shift[:, m:m + 1],
                                scale=norms[n].rs[:, m:m + 1])
                last.then_inc(s_out, 1)

            def constants_1():
                act.wait_ge(w_in[1], 16 * n_parameters[1])
                copy(w1h[:, :, :], w1_raw).then_inc(c_w1h, 1)
                act.wait_ge(c_gc, 1)
                copy(gh[:, :, 0:F], g_raw[:, :, :]).then_inc(c_gh, 1)

            def constants_23():
                act.wait_ge(c_m2, 1)
                act.wait_ge(w_in[2], 16 * n_parameters[2])
                copy(w2h[:, :, :], l2_raw[:, :, :]).then_inc(c_w2h, 1)
                act.wait_ge(c_u3, 1)
                act.wait_ge(w_in[3], 16 * n_parameters[3])
                copy(w3h[:, :, :], w3_raw[:, :, :]).then_inc(c_w3h, 1)

            def l0_split_x(b):
                act.wait_ge(xt_in[b.slot(2)], b.dma_done(2))
                if b.follows(1):
                    act.wait_ge(s_y0mm, b.count(KN, 0))
                copy(x0th[:, :, :], xt[:, b.slot(2), :, :]).then_inc(s_x0th, 1)

            def l0_split_at(b):
                s = b.slot(RING)
                act.wait_ge(at_in[s], b.dma_done(RING))
                copy(ath[:, s, :, :], at[:, s, :, :]).then_inc(s_ath, 1)

            def l0_z(b):
                for m, ps in enumerate((A0, B0)):
                    act.wait_ge(s_y0mm, b.count(KN, m + 1))
                    if m == 0:
                        reuse(act, s_azmm, b)
                        reuse(act, s_x1, b)
                    copy(zh[:, m, 0:F], ps[:, F:2 * F])
                    copy(t0[:, m, :], ps[:, 0:F]).then_inc(s_zh, 1)

            def l0_x1(b):
                reuse(act, s_x1b, b)
                reuse(act, s_x1l, b)
                normalise(0, x1, s_x1, b)

            def l0_x1h(b):
                ready(act, s_x1, b)
                reuse(act, s_sxmm, b)
                copy(x1h[:, :, :], x1[:, :, :]).then_inc(s_x1h, 1)

            def l0_hbh(b):
                ready(act, s_hb, b)
                reuse(act, s_smm, b)
                copy(hbh[:, :, :], hb[:, :, :]).then_inc(s_hbh, 1)

            def l1_sh(b):
                ready(act, s_smm, b)
                if b.follows(2):
                    act.wait_ge(s_ymm, b.before(1))
                copy(sh[:, b.slot(2), :, :], tiles(B0)).then_inc(s_sh, 1)

            def l1_sxh(b):
                ready(act, s_sxmm, b)
                if b.follows(1):
                    act.wait_ge(s_rmm, b.count(2, 0))
                copy(sxh[:, :, :], tiles(B1)).then_inc(s_sxh, 1)

            def l1_r1(b):
                reuse(act, s_r1l, b)
                reuse(act, s_r1l2, b)
                for m in range(KH):
                    if m % 2 == 0:
                        act.wait_ge(s_rmm, b.count(2, m // 2 + 1))
                    last = nc.scalar.activation(r1[:, m, :], tiles((A1, B1)[m // 2])[:, m % 2, :], ACT.Relu,
                                                bias=b1c[:, m:m + 1])
                    if m % 2:
                        last.then_inc(s_r1, 1)

            def l1_sq(b):
                if b.is_first:
                    act.wait_ge(c_g, 1)
                reuse(act, s_sq1, b)
                for m in range(2):
                    act.wait_ge(s_r1, b.count(2, m + 1))
                    c = slice(2 * m, 2 * m + 2)
                    last = nc.scalar.activation(sq[:, c, :], r1[:, c, :], ACT.Square)
                last.then_inc(s_sq, 1)

            def l1_r1h(b):
                reuse(act, s_vmm, b)
                for m in range(2):
                    act.wait_ge(s_r1, b.count(2, m + 1))
                    copy(r1h[:, 2 * m:2 * m + 2, :], r1[:, 2 * m:2 * m + 2, :]).then_inc(s_r1h2, 1)

            def l1_uh(b):
                ready(act, s_u, b)
                reuse(act, s_ymm, b)
                copy(uh[:, :, :], u[:, :, :]).then_inc(s_uh, 1)

            def l1_x2(b):
                normalise(1, x2[:, b.slot(2), :, :], s_x2, b)

            def l1_x2mh(b):
                ready(act, s_x2, b)
                reuse(act, s_aggmm, b)
                for m in range(KN):
                    last = copy(x2mh[:, m, :], x2[:, b.slot(2), m, :], scale=mask_of(b, m))
                last.then_inc(s_x2mh, 1)

            def l2_x2th(b):
                ready(act, s_x2tr, b)
                if b.follows(1):
                    act.wait_ge(s_qvmm, b.count(KN, 0))
                copy(x2th[:, :, :], tiles(A2)).then_inc(s_x2th, 1)

            def l2_qv(b):
                reuse(act, s_x3, b)
                for m, ps in enumerate((B2, A2)):
                    act.wait_ge(s_qvmm, b.count(KN, m + 1))
                    last = copy(qv[:, m, :], ps[:, :])
                last.then_inc(s_qv, 1)

            def l2_exp(b):
                ready(act, s_nmx, b)
                nc.scalar.activation(ew[:, :], wdot[:, :], ACT.Exp, bias=nmx[:, 0:1], scale=-1.0)
                nc.scalar.activation(ejunk[:, :], A2[:, 0:N], ACT.Exp, bias=nmx[:, 0:1], scale=-1.0,
                                     accum_out=esum[:, 0:1]).then_inc(s_esum, 1)

            def l2_x3(b):
                normalise(2, x3[:, b.slot(2), :, :], s_x3, b)

            def l3_x3th(b):
                ready(act, s_x3tr, b)
                if b.follows(1):
                    act.wait_ge(s_y01mm, b.count(KN, 0))
                copy(x3th[:, :, :], tiles(B2)).then_inc(s_x3th, 1)

            def l3_y2h(b):
                reuse(act, s_p2mm, b)
                for m, ps in enumerate((B3, A3)):
                    act.wait_ge(s_y2mm, b.count(KN, m + 1))
                    last = copy(y2h[:, m, 0:F], ps[:, 0:F])
                last.then_inc(s_y2h, 1)

            def l3_ez(b):
                ready(act, s_sitr, b)
                reuse(act, s_all, b)
                for m in range(KN):
                    last = copy(al[:, m, :], B3[:, 0:N], bias=sj[:, m:m + 1])
                last.then_inc(s_ez, 1)

            def l3_exp(b):
                ready(act, s_el, b)
                nc.scalar.activation(al[:, :, :], al[:, :, :], ACT.Exp).then_inc(s_ee, 1)

            def l3_alh(b):
                ready(act, s_al, b)
                reuse(act, s_p1mm, b)
                copy(alh[:, :, :], al[:, :, :]).then_inc(s_alh, 1)

            def l3_y01(b):
                reuse(act, s_z3l, b)
                reuse(act, s_xo, b)
                for m, ps in enumerate((A3, B3)):
                    act.wait_ge(s_y01mm, b.count(KN, m + 1))
                    last = copy(y01[:, m, :], ps[:, :])
                last.then_inc(s_y01, 1)

            def l3_z3h(b):
                ready(act, s_z3, b)
                reuse(act, s_p1mm, b)
                copy(z3h[:, :, :], z3).then_inc(s_z3h, 1)

            def l3_out(b):
                if b.follows(2):
                    act.wait_ge(stored[b.slot(2)], b.dma_done(2) - 16)
                normalise(3, xo[:, b.slot(2), :, :], s_xo, b)

            stages = [
                (l3_alh, 3), (guess, 0, 0), (l0_split_x, -1), (l1_uh, 1), (l3_y01, 3), (l1_sh, 0), (l2_exp, 2),
                (l0_x1, 0), (l0_split_at, -1), (l0_x1h, 0), (l3_z3h, 3), (log_var, 2, 2), (guess, 2, 2),
                (l0_z, -1), (log_var, 1, 1), (guess, 1, 1), (l1_sxh, 0), (l2_x3, 2), (l1_x2, 1), (l3_x3th, 2),
                (l2_x2th, 1), (l1_x2mh, 1), (l1_r1, 0), (l3_y2h, 2), (log_var, 3, 3), (l1_r1h, 0),
                (guess, 3, 3), (l1_sq, 0), (l2_qv, 1), (l3_ez, 2), (l0_hbh, -1), (l3_exp, 2), (l3_out, 3),
                (log_var, HIDDEN, 0), (guess, HIDDEN, 0), (log_var, 0, -1),
            ]

            nc.scalar.preload_act_table_set("natural_log_exp_and_others")
            act.wait_ge(w_in[0], 16 * n_parameters[0])
            copy(w0h[:, :, :], w0_raw).then_inc(c_w0h, 1)
            steps_of(act, stages, {l0_z: constants_1, l1_sxh: constants_23})

        @block.vector
        def _(dve):
            v = nc.vector

            def row_stats(n, b):
                ready(dve, norms[n].s_t, b)
                for m in range(KN):
                    last = v.bn_stats(norms[n].bn[:, m, :], norms[n].t[:, m, :])
                last.then_inc(norms[n].s_bn, 1)

            def mean_var(n, b):
                dve.wait_ge(s_memset, 1)
                ready(dve, norms[n].s_bn, b)
                for m in range(KN):
                    last = v.bn_aggr(norms[n].mv[:, m, :], norms[n].bn[:, m, :])
                last.then_inc(norms[n].s_mv.sem, 1)

            def newton_1(n, b):
                ready(dve, norms[n].s_guess, b)
                v.scalar_tensor_tensor(norms[n].va[:, :], norms[n].var, EPS_LN, norms[n].guess[:, :],
                                       ALU.add, ALU.mult).then_inc(norms[n].s_va.sem, 1)

            def newton_2(n, b):
                ready(dve, norms[n].s_va, b)
                v.tensor_tensor(norms[n].va[:, :], norms[n].va[:, :], norms[n].guess[:, :],
                                ALU.mult).then_inc(norms[n].s_vaa.sem, 1)

            def newton_3(n, b):
                ready(dve, norms[n].s_vaa, b)
                v.scalar_tensor_tensor(norms[n].rs[:, :], norms[n].va[:, :], NEWTON_S, norms[n].guess[:, :],
                                       ALU.subtract, ALU.mult, reverse0=True).then_inc(norms[n].s_rs.sem, 1)

            def shift(n, b):
                ready(dve, norms[n].s_rs, b)
                v.scalar_tensor_tensor(norms[n].shift[:, :], norms[n].mean, -1.0, norms[n].rs[:, :],
                                       ALU.mult, ALU.mult).then_inc(norms[n].s_shift.sem, 1)

            def low(out, whole, high):
                return v.tensor_tensor(out, whole, f(high), ALU.subtract)

            def constants_0():
                v.memset(ones[:, :], 1.0)
                v.memset(ln_a[:, :], math.log(NEWTON_A))
                for t, val in ((zh, 1.0), (zl, 0.0), (y2h, 1.0), (y2l, 0.0), (gh, 1.0), (gl, 0.0)):
                    v.memset(f(t[:, :, F:NO]), val)
                v.memset(eps_ln[:, :], EPS_LN).then_inc(s_memset, 1)
                dve.wait_ge(c_w0h, 1)
                low(w0l[:, :, :], w0_raw, w0h[:, :, :]).then_inc(c_w0, 1)

            def constants_1():
                dve.wait_ge(w_in[1], 16 * n_parameters[1])
                for k in range(KH):
                    last = v.tensor_scalar(g_raw[:, k, :], w2_raw[:, k, :], gammac[:, k:k + 1], None, ALU.mult)
                last.then_inc(c_gamma, 1)
                dve.wait_ge(s_memset, 1)
                for k in range(KH):
                    last = v.tensor_scalar(beta_b[:, k, :], ones[:, :], betac[:, k:k + 1], None, ALU.mult)
                last.then_inc(c_beta, 1)
                for k in range(KF):
                    last = v.tensor_scalar(bv_b[:, k, :], ones[:, :], bvc[:, k:k + 1], None, ALU.mult)
                last.then_inc(c_bv, 1)

            def constants_centre():
                dve.wait_ge(c_w1h, 1)
                low(w1l[:, :, :], w1_raw, w1h[:, :, :]).then_inc(c_w1, 1)
                dve.wait_ge(c_mean, 1)
                v.tensor_scalar(g_mean, A1[:, 0:F], 1.0 / H1, None, ALU.mult).then_inc(c_gmean, 1)
                dve.wait_ge(c_gmean, 1)
                dve.wait_ge(c_gamma, 1)
                for k in range(KH):
                    last = v.tensor_tensor(g_raw[:, k, :], g_raw[:, k, :], g_mean, ALU.subtract)
                last.then_inc(c_gc, 1)
                dve.wait_ge(c_c2mm, 1)
                v.tensor_copy(c2[:, :], B1[:, 0:F]).then_inc(c_c2, 1)

            def constants_23():
                dve.wait_ge(c_m, 1)
                v.tensor_scalar(l2_raw[:, :, 0:F], tiles(A2), -float(F) ** -0.5, None, ALU.mult).then_inc(c_m2, 1)
                dve.wait_ge(c_u, 1)
                for m in range(KF):
                    last = v.tensor_copy(w3_raw[:, m, 3 * F:3 * F + 2], A3[:, 2 * m:2 * m + 2])
                last.then_inc(c_u3, 1)
                dve.wait_ge(w_in[3], 16 * n_parameters[3])
                v.tensor_scalar(b2_half[:, :], b2_half[:, :], 0.5, None, ALU.mult)
                v.tensor_tensor(bk_sum[:, :], bk_raw[:, 0, :], bk_raw[:, 1, :], ALU.add)
                dve.wait_ge(c_e, 1)
                v.tensor_copy(e_const[:, :], B3[:, 0:2]).then_inc(c_sum, 1)
                dve.wait_ge(c_sum, 1)
                v.tensor_tensor(bk_sum[:, :], bk_sum[:, :], bk_raw[:, 2, :], ALU.add)
                v.tensor_tensor(e_bias[:, :], e_const[:, 0:1], e_const[:, 1:2], ALU.add).then_inc(c_sum, 1)
                dve.wait_ge(c_sum, 2)
                v.tensor_tensor(e_bias[:, :], e_bias[:, :], ab_b[:, :], ALU.add).then_inc(c_bias, 1)

            def split_w2():
                dve.wait_ge(c_w2h, 1)
                low(w2l[:, :, :], l2_raw[:, :, :], w2h[:, :, :]).then_inc(c_w2, 1)

            def split_w3():
                dve.wait_ge(c_w3h, 1)
                low(w3l[:, :, :], w3_raw[:, :, :], w3h[:, :, :]).then_inc(c_w3, 1)

            def l0_h(b):
                s, h = b.slot(RING), b.slot(2)
                dve.wait_ge(at_in[s], b.dma_done(RING))
                for k in range(KN):
                    last = v.tensor_scalar(ht[:, h, k, :], at[:, s, k, :], 0.0, None, ALU.not_equal, ALU.add,
                                           accum_out=cnt[:, k:k + 1])
                last.then_inc(s_ht, 1)

            def l0_edge_floor(b):
                ready(dve, s_ht, b)
                v.tensor_scalar(be0[:, :], cnt[:, :], 1.0, None, ALU.max).then_inc(s_cntmax.sem, 1)

            def l0_edge_recip(b):
                ready(dve, s_cntmax, b)
                v.reciprocal(be[:, :], be0[:, :]).then_inc(s_be.sem, 1)

            def l0_zl(b):
                for m, ps in enumerate((A0, B0)):
                    dve.wait_ge(s_zh, b.count(KN, m + 1))
                    last = low(zl[:, m, 0:F], ps[:, F:2 * F], zh[:, m, 0:F])
                last.then_inc(s_zl, 1)

            def l0_degree(b):
                ready(dve, s_azmm, b)
                ready(dve, s_dnmm, b)
                for m, ps in enumerate((A0, B0)):
                    last = v.tensor_scalar(deg[:, m:m + 1], ps[:, F:F + 1], EPS_DEG, None, ALU.max)
                last.then_inc(s_deg.sem, 1)

            def l0_degree_recip(b):
                ready(dve, s_deg, b)
                v.reciprocal(rdeg[:, :], deg[:, :]).then_inc(s_rdeg.sem, 1)

            def l0_r(b):
                ready(dve, s_rdeg, b)
                for m, ps in enumerate((A0, B0)):
                    last = v.scalar_tensor_tensor(t0[:, m, :], ps[:, 0:F], rdeg[:, m:m + 1], t0[:, m, :],
                                                  ALU.mult, ALU.add)
                last.then_inc(s_r0, 1)

            def l0_t(b):
                s = b.slot(RING)
                ready(dve, s_r0, b)
                dve.wait_ge(xm_in[s], b.dma_done(RING))
                v.scalar_tensor_tensor(t0[:, :, :], t0[:, :, :], 0.0,
                                       xm[:, s, 0:KN * F].rearrange("p (m f) -> p m f", f=F),
                                       ALU.max, ALU.add).then_inc(s_t0, 1)

            def l0_dn(b):
                ready(dve, s_dnmm, b)
                ready(dve, s_azmm, b)
                v.tensor_reduce(dn[:, :], DN, AX.X, ALU.add).then_inc(s_dn.sem, 1)

            def l0_dn_floor(b):
                ready(dve, s_dn, b)
                v.tensor_scalar(dmax[:, :], dn[:, :], TINY, None, ALU.max).then_inc(s_dmax.sem, 1)

            def l0_dn_recip(b):
                ready(dve, s_dmax, b)
                v.reciprocal(drec[:, :], dmax[:, :]).then_inc(s_drec.sem, 1)

            def l0_dnb(b):
                ready(dve, s_drec, b)
                for m in range(KN):
                    last = v.scalar_tensor_tensor(dnb[:, m, :], dn[:, m:m + 1].to_broadcast([P, P]), 0.0,
                                                  drec[:, m:m + 1].to_broadcast([P, P]), ALU.is_gt, ALU.mult)
                last.then_inc(s_dnb, 1)

            def l0_hb(b):
                ready(dve, s_dntr, b)
                ready(dve, s_be, b)
                h = b.slot(2)
                for k in range(KN):
                    last = v.scalar_tensor_tensor(hb[:, k, :], f(ht[:, h, k, :]), be[:, k:k + 1], B0[:, 0:N],
                                                  ALU.mult, ALU.mult)
                last.then_inc(s_hb, 1)

            def l1_sl(b):
                ready(dve, s_sh, b)
                low(sl[:, b.slot(2), :, :], tiles(B0), sh[:, b.slot(2), :, :]).then_inc(s_sl, 1)

            def l1_sxl(b):
                ready(dve, s_sxh, b)
                low(sxl[:, :, :], tiles(B1), sxh[:, :, :]).then_inc(s_sxl, 1)

            def l1_r1l(b):
                dve.wait_ge(s_r1h2, b.count(2, 2))
                low(r1l[:, 2:4, :], r1[:, 2:4, :], r1h[:, 2:4, :]).then_inc(s_r1l, 1)

            def l1_hidden_mean(b):
                ready(dve, s_vmm, b)
                for m, ps in enumerate((A1, B1)):
                    last = v.tensor_scalar(mu1[:, m:m + 1], ps[:, F:F + 1], 1.0 / H1, None, ALU.mult)
                last.then_inc(s_mu.sem, 1)

            def l1_hidden_mean_square(b):
                ready(dve, s_mu, b)
                v.tensor_tensor(mq1[:, :], mu1[:, :], mu1[:, :], ALU.mult).then_inc(s_mq.sem, 1)

            def l1_hidden_var(b):
                ready(dve, s_mq, b)
                for m, ps in enumerate((A1, B1)):
                    last = v.scalar_tensor_tensor(var1[:, m:m + 1], ps[:, NO:NO + 1], 1.0 / H1, mq1[:, m:m + 1],
                                                  ALU.mult, ALU.subtract)
                last.then_inc(s_var.sem, 1)

            def l1_hidden_var_floor(b):
                ready(dve, s_var, b)
                v.tensor_scalar(vc1[:, :], var1[:, :], 0.0, None, ALU.max).then_inc(norms[HIDDEN].s_mv.sem, 1)

            def l1_u(b):
                if b.is_first:
                    dve.wait_ge(c_c2, 1)
                ready(dve, norms[HIDDEN].s_rs, b)
                for m, ps in enumerate((A1, B1)):
                    last = v.scalar_tensor_tensor(u[:, m, :], ps[:, 0:F], norms[HIDDEN].rs[:, m:m + 1], c2[:, :],
                                                  ALU.mult, ALU.add)
                last.then_inc(s_u, 1)

            def l1_t(b):
                ready(dve, s_ymm, b)
                ready(dve, s_x1b, b)
                v.scalar_tensor_tensor(t1[:, :, :], t1[:, :, :], 2.0, tiles(A1), ALU.mult, ALU.add).then_inc(s_t1, 1)

            def l1_x2ml(b):
                ready(dve, s_x2mh, b)
                for m in range(KN):
                    last = v.scalar_tensor_tensor(x2ml[:, m, :], x2[:, b.slot(2), m, :], mask_of(b, m),
                                                  f(x2mh[:, m, :]), ALU.mult, ALU.subtract)
                last.then_inc(s_x2ml, 1)

            def l2_x2tl(b):
                ready(dve, s_x2th, b)
                low(x2tl[:, :, :], tiles(A2), x2th[:, :, :]).then_inc(s_x2tl, 1)

            def l2_w(b):
                ready(dve, s_aggmm, b)
                ready(dve, s_qv, b)
                for m in range(KN):
                    last = v.scalar_tensor_tensor(qv[:, m, 0:F], tiles(B2)[:, m, :], mask_of(b, m), qv[:, m, 0:F],
                                                  ALU.mult, ALU.mult, accum_out=wdot[:, m:m + 1])
                last.then_inc(s_w2, 1)

            def l2_wb(b):
                ready(dve, s_w2, b)
                v.tensor_copy(wb[:, :, :], wdot[:, :].unsqueeze(2).to_broadcast([P, KN, P])).then_inc(s_wb, 1)

            def l2_max(b):
                ready(dve, s_wtr, b)
                v.tensor_reduce(nmx[:, :], A2[:, 0:N], AX.X, ALU.min).then_inc(s_nmx, 1)

            def l2_sum_recip(b):
                ready(dve, s_esum, b)
                v.reciprocal(ercp[:, :], esum[:, :]).then_inc(s_ercp.sem, 1)

            def l2_softmax(b):
                ready(dve, s_ercp, b)
                v.tensor_scalar(aw[:, :], ew[:, :], ercp[:, 0:1], None, ALU.mult).then_inc(s_a.sem, 1)

            def l2_t(b):
                ready(dve, s_a, b)
                for m in range(KN):
                    last = v.scalar_tensor_tensor(t2[:, m, :], t2[:, m, :], aw[:, m:m + 1],
                                                  x2[:, b.slot(2), m, :], ALU.mult, ALU.add)
                last.then_inc(s_t2, 1)

            def l3_x3tl(b):
                ready(dve, s_x3th, b)
                low(x3tl[:, :, :], tiles(B2), x3th[:, :, :]).then_inc(s_x3tl, 1)

            def l3_sib(b):
                if b.is_first:
                    dve.wait_ge(c_bias, 1)
                """Both halves of the attention's logits: sj + c, and si spread along the free axis."""
                ready(dve, s_y2h, b)
                reuse(dve, s_ez, b)
                for m, ps in enumerate((B3, A3)):
                    v.tensor_scalar(sj[:, m:m + 1], ps[:, F:F + 1], e_bias[:, 0:1], None, ALU.add)
                    last = v.tensor_copy(sib[:, m, :], ps[:, F + 1:F + 2].to_broadcast([P, P]))
                last.then_inc(s_sib, 1)

            def l3_y2l(b):
                ready(dve, s_y2h, b)
                for m, ps in enumerate((B3, A3)):
                    last = low(y2l[:, m, 0:F], ps[:, 0:F], y2h[:, m, 0:F])
                last.then_inc(s_y2l, 1)

            def l3_leaky(b):
                ready(dve, s_ez, b)
                v.scalar_tensor_tensor(al[:, :, :], al[:, :, :], SLOPE, al[:, :, :],
                                       ALU.mult, ALU.max).then_inc(s_el, 1)

            def l3_row_sum(b):
                ready(dve, s_p2mm, b)
                for m, ps in enumerate((A3, B3)):
                    last = v.tensor_scalar(rsum[:, m:m + 1], ps[:, F:F + 1], EPS_SUM, None, ALU.add)
                last.then_inc(s_rsum.sem, 1)

            def l3_row_recip(b):
                ready(dve, s_rsum, b)
                v.reciprocal(rrec[:, :], rsum[:, :]).then_inc(s_rrec.sem, 1)

            def l3_z3(b):
                ready(dve, s_rrec, b)
                for m, ps in enumerate((A3, B3)):
                    last = v.scalar_tensor_tensor(z3[:, m, :], ps[:, 0:F], rrec[:, m:m + 1], z3[:, m, :],
                                                  ALU.mult, ALU.add)
                last.then_inc(s_z3, 1)

            def l3_r(b):
                ready(dve, s_p1mm, b)
                ready(dve, s_y0b, b)
                for m in range(KN):
                    last = v.scalar_tensor_tensor(t3[:, m, :], tiles(A3)[:, m, :], rrec[:, m:m + 1], t3[:, m, :],
                                                  ALU.mult, ALU.add)
                last.then_inc(s_r3, 1)

            def l3_t(b):
                ready(dve, s_r3, b)
                v.scalar_tensor_tensor(t3, t3, 0.0, x3[:, b.slot(2), :, :],
                                       ALU.max, ALU.add).then_inc(s_t3, 1)

            stages = [
                (shift, 0, 0), (l2_max, 2), (l1_sl, 0), (l2_sum_recip, 2), (l2_softmax, 2), (l2_t, 2),
                (l3_row_sum, 3), (l3_row_recip, 3), (row_stats, 2, 2), (l3_z3, 3), (l1_t, 1), (mean_var, 2, 2),
                (row_stats, 1, 1), (l0_h, -1), (newton_1, 2, 2), (mean_var, 1, 1), (newton_2, 2, 2),
                (l0_zl, -1), (newton_3, 2, 2), (shift, 2, 2), (l0_edge_floor, -1), (newton_1, 1, 1),
                (newton_2, 1, 1), (l0_edge_recip, -1), (newton_3, 1, 1), (shift, 1, 1), (l1_sxl, 0),
                (l0_dn, -1), (l0_degree, -1), (l3_r, 3), (l3_x3tl, 2), (l0_dn_floor, -1), (l3_t, 3),
                (l2_x2tl, 1), (l0_degree_recip, -1), (l0_dn_recip, -1), (row_stats, 3, 3), (l0_r, -1),
                (mean_var, 3, 3), (l0_dnb, -1), (l3_y2l, 2), (l3_sib, 2), (l1_r1l, 0), (l0_t, -1),
                (newton_1, 3, 3), (l1_x2ml, 1), (newton_2, 3, 3), (l0_hb, -1), (newton_3, 3, 3), (l3_leaky, 2),
                (shift, 3, 3), (row_stats, 0, -1), (l1_hidden_mean, 0), (l1_hidden_mean_square, 0),
                (l1_hidden_var, 0), (l1_hidden_var_floor, 0), (mean_var, 0, -1), (newton_1, HIDDEN, 0),
                (newton_2, HIDDEN, 0), (newton_3, HIDDEN, 0), (l1_u, 0), (l2_w, 1), (newton_1, 0, -1),
                (l2_wb, 1), (newton_2, 0, -1), (newton_3, 0, -1),
            ]

            constants_0()
            steps_of(dve, stages, {l0_h: constants_1, l0_zl: constants_centre, l1_sl: constants_23,
                                   l1_u: split_w2, l1_t: split_w3})

        @block.gpsimd
        def _(pool):
            g = nc.gpsimd

            def l0_split_at(b):
                s = b.slot(RING)
                ready(pool, s_ath, b)
                g.tensor_tensor(atl[:, s, :, :], at[:, s, :, :], f(ath[:, s, :, :]), ALU.subtract).then_inc(s_atl, 1)
                ready(pool, s_atl, b)
                reuse(pool, s_dnmm, b)
                first, first_l = at[:, s, :, 0:1], f(atl[:, s, :, 0:1])
                g.tensor_tensor(wcol[:, :, 0:1], first, first_l, ALU.subtract)
                g.tensor_tensor(wcol[:, :, 1:2], first, f(ath[:, s, :, 0:1]), ALU.subtract).then_inc(s_wcol, 1)

            def low(out, whole, high):
                return g.tensor_tensor(out, whole, f(high), ALU.subtract)

            def constants():
                pool.wait_ge(c_gh, 1)
                low(gl[:, :, 0:F], g_raw[:, :, :], gh[:, :, 0:F]).then_inc(c_g, 1)

            def l0_hbl(b):
                ready(pool, s_hbh, b)
                low(hbl[:, :, :], hb[:, :, :], hbh[:, :, :]).then_inc(s_hbl, 1)

            def l0_split_x(b):
                ready(pool, s_x0th, b)
                low(x0tl[:, :, :], xt[:, b.slot(2), :, :], x0th[:, :, :]).then_inc(s_x0tl, 1)

            def l0_x1l(b):
                ready(pool, s_x1h, b)
                low(x1l[:, :, :], x1[:, :, :], x1h[:, :, :]).then_inc(s_x1l, 1)

            def l1_r1l(b):
                pool.wait_ge(s_r1h2, b.count(2, 1))
                low(r1l[:, 0:2, :], r1[:, 0:2, :], r1h[:, 0:2, :]).then_inc(s_r1l2, 1)

            def l1_ul(b):
                ready(pool, s_uh, b)
                low(ul[:, :, :], u[:, :, :], uh[:, :, :]).then_inc(s_ul, 1)

            def l3_alpha(b):
                ready(pool, s_ee, b)
                g.tensor_tensor(al[:, :, :], al[:, :, :], at[:, b.slot(RING), :, :], ALU.mult).then_inc(s_al, 1)

            def l3_all(b):
                ready(pool, s_alh, b)
                low(all_[:, :, :], al[:, :, :], alh[:, :, :]).then_inc(s_all, 1)

            def l3_z3l(b):
                ready(pool, s_z3h, b)
                low(z3l[:, :, :], z3, z3h[:, :, :]).then_inc(s_z3l, 1)

            def l1_x1b(b):
                if b.is_first:
                    pool.wait_ge(c_bias, 1)
                ready(pool, s_x1, b)
                reuse(pool, s_x2, b)
                g.tensor_tensor(t1[:, :, :], x1[:, :, :], b2_half[:, :].unsqueeze(1).to_broadcast([P, KN, F]),
                                ALU.add).then_inc(s_x1b, 1)

            def l1_sumsq(b):
                ready(pool, s_sq, b)
                g.tensor_tensor(sq[:, 0:2, :], sq[:, 0:2, :], sq[:, 2:4, :], ALU.add).then_inc(s_sq2, 1)
                ready(pool, s_sq2, b)
                reuse(pool, s_vmm, b)
                g.tensor_tensor(sq1[:, :], sq[:, 0, :], sq[:, 1, :], ALU.add).then_inc(s_sq1, 1)

            def l3_y0b(b):
                if b.is_first:
                    pool.wait_ge(c_bias, 1)
                ready(pool, s_y01, b)
                g.tensor_tensor(t3, t3, bk_sum[:, :].unsqueeze(1).to_broadcast([P, KN, F]), ALU.add).then_inc(s_y0b, 1)

            stages = [
                (l1_ul, 1), (l0_split_x, -1), (l3_y0b, 3), (l0_x1l, 0), (l3_z3l, 3), (l0_split_at, -1),
                (l1_r1l, 0), (l1_sumsq, 0), (l1_x1b, 0), (l3_alpha, 2), (l0_hbl, -1), (l3_all, 2),
            ]

            steps_of(pool, stages, {l0_split_at: constants})


def kernel(x, adj, nodemask, L0_gnn_W, L1_gnn_W1, L1_gnn_b1, L1_gnn_gamma, L1_gnn_beta, L1_gnn_W2, L1_gnn_b2,
           L2_gnn_Wqk, L2_gnn_Wv, L3_gnn_Wv, L3_gnn_bv, L3_gnn_aw, L3_gnn_ab, L3_gnn_Wk, L3_gnn_bk):
    import numpy as np
    import concourse.bacc as bacc
    from concourse.bass_utils import run_bass_kernel_spmd

    def rows(a):
        a = np.asarray(a)
        k = a.shape[-2] // P
        a = a.reshape(a.shape[:-2] + (k, P, a.shape[-1]))
        return np.ascontiguousarray(np.moveaxis(a, -3, -2))

    def column(a):
        return np.ascontiguousarray(np.asarray(a).reshape(-1, P).T)

    x, adj, nodemask = np.asarray(x), np.asarray(adj), np.asarray(nodemask)
    W, Wk = np.asarray(L0_gnn_W).T, np.asarray(L3_gnn_Wk)
    aw = np.asarray(L3_gnn_aw)[:, 0].reshape(2, KF, P)
    arrays = {
        "at": rows(np.swapaxes(adj, 1, 2)),
        "xt": rows(np.swapaxes(x, 1, 2)),
        "xm": np.concatenate([rows(x).reshape(B, P, KN * F),
                              np.swapaxes(nodemask.reshape(B, KN, P), 1, 2)], axis=2),
        "w_l0": rows(np.concatenate([W[0:F], W[F:2 * F]], axis=1)),
        "w1": rows(np.asarray(L1_gnn_W1).T),
        "w2": rows(np.asarray(L1_gnn_W2).T),
        "wqk": rows(np.asarray(L2_gnn_Wqk).T),
        "wv2": rows(L2_gnn_Wv),
        "w3": rows(np.concatenate([Wk[0], Wk[1], Wk[2]], axis=1)),
        "wv3": rows(np.asarray(L3_gnn_Wv).T),
        "aw": np.ascontiguousarray(np.transpose(aw, (2, 1, 0))),
        "cols": np.concatenate([column(L1_gnn_b1), column(L1_gnn_gamma), column(L1_gnn_beta),
                                column(L3_gnn_bv)], axis=1),
        "b2": np.ascontiguousarray(np.broadcast_to(np.asarray(L1_gnn_b2), (P, F))),
        "bk": np.ascontiguousarray(np.broadcast_to(np.asarray(L3_gnn_bk), (P, 3, F))),
        "ab": np.ascontiguousarray(np.broadcast_to(np.asarray(L3_gnn_ab), (P, 1))),
        "ident": np.eye(P, dtype=np.float32),
    }
    nc = bacc.Bacc("TRN2", target_bir_lowering=False, num_devices=1)
    arrays = {f"in_{k}": np.ascontiguousarray(a) for k, a in arrays.items()}
    args = [nc.dram_tensor(k, a.shape, mybir.dt.from_np(a.dtype), kind="ExternalInput").ap() for k, a in arrays.items()]
    args.append(nc.dram_tensor("out", (B, P, KN, F), F32, kind="ExternalOutput").ap())
    resnorm_kernel(nc, *args)
    r = run_bass_kernel_spmd(nc, [arrays], core_ids=[0])
    out = r.results[0]["out"]
    return np.ascontiguousarray(np.moveaxis(out, 2, 1).reshape(B, N, F))
```
